# Optimizing a Trainium2 kernel written in Bass

```python
import numpy as np
import jax
import jax.numpy as jnp

def _softmax(x, axis=-1):
    return jax.nn.softmax(x, axis=axis)

def _gelu(x):
    return jax.nn.gelu(x, approximate=True)

def _silu(x):
    return jax.nn.silu(x)

def _sigmoid(x):
    return jax.nn.sigmoid(x)

def _layernorm(x, axis=-1, eps=1e-05):
    m = jnp.mean(x, axis=axis, keepdims=True)
    v = jnp.var(x, axis=axis, keepdims=True)
    return (x - m) / jnp.sqrt(v + eps)

def _scatter_add(tgt, idx, src, axis=0):
    return tgt.at[idx].add(src)

def _segment_sum(src, seg, n):
    return jax.ops.segment_sum(src, seg, n)
kernel_name = 'mk_macaron_d2_jaxref_r8_ab7d76'

def setup_inputs(seed: int=0):
    np.random.seed(seed)
    _w = jnp.asarray

    def _L0_attn_setup():
        import jax, jax.numpy as jnp
        import numpy as np
        EMBED_DIM = 256
        NUM_HEADS = 16
        HEAD_DIM = EMBED_DIM // NUM_HEADS
        B, T = (4, 256)
        key = jax.random.key(seed)
        ks = jax.random.split(key, 9)
        s = 1.0 / np.sqrt(EMBED_DIM)
        x = jax.random.normal(ks[0], (B, T, EMBED_DIM), dtype=jnp.float32)
        Wq = jax.random.normal(ks[1], (EMBED_DIM, EMBED_DIM), dtype=jnp.float32) * s
        bq = jnp.zeros((EMBED_DIM,), dtype=jnp.float32)
        Wk = jax.random.normal(ks[2], (EMBED_DIM, EMBED_DIM), dtype=jnp.float32) * s
        bk = jnp.zeros((EMBED_DIM,), dtype=jnp.float32)
        Wv = jax.random.normal(ks[3], (EMBED_DIM, EMBED_DIM), dtype=jnp.float32) * s
        bv = jnp.zeros((EMBED_DIM,), dtype=jnp.float32)
        Wo = jax.random.normal(ks[4], (EMBED_DIM, EMBED_DIM), dtype=jnp.float32) * s
        bo = jnp.zeros((EMBED_DIM,), dtype=jnp.float32)
        return {'x': x, 'Wq': Wq, 'bq': bq, 'Wk': Wk, 'bk': bk, 'Wv': Wv, 'bv': bv, 'Wo': Wo, 'bo': bo}
    _L0_attn_in = _L0_attn_setup()

    def _L0_ffn_setup():
        import jax, jax.numpy as jnp
        import numpy as np
        TOP_K = 4
        key = jax.random.key(seed)
        ks = jax.random.split(key, 8)
        B, S, D, E, H, HS = (2, 256, 256, 16, 128, 512)
        scaled = lambda k, shape, fan: jax.random.normal(k, shape, jnp.float32) * fan ** (-0.5)
        return {'x': jax.random.normal(ks[0], (B, S, D), jnp.float32), 'w_router': scaled(ks[1], (D, E), D), 'we1': scaled(ks[2], (E, D, H), D), 'we3': scaled(ks[3], (E, D, H), D), 'we2': scaled(ks[4], (E, H, D), H), 'ws1': scaled(ks[5], (D, HS), D), 'ws3': scaled(ks[6], (D, HS), D), 'ws2': scaled(ks[7], (HS, D), HS)}
    _L0_ffn_in = _L0_ffn_setup()

    def _L1_attn_setup():
        import jax, jax.numpy as jnp
        import numpy as np
        import math
        NUM_HEADS = 16
        key = jax.random.key(seed)
        ks = jax.random.split(key, 5)
        B, S, D = (2, 256, 256)
        scale = 1.0 / math.sqrt(D)
        return {'x': jax.random.normal(ks[0], (B, S, D), dtype=jnp.float32), 'Wq': jax.random.normal(ks[1], (D, D), dtype=jnp.float32) * scale, 'Wk': jax.random.normal(ks[2], (D, D), dtype=jnp.float32) * scale, 'Wv': jax.random.normal(ks[3], (D, D), dtype=jnp.float32) * scale, 'Wp': jax.random.normal(ks[4], (D, D), dtype=jnp.float32) * scale}
    _L1_attn_in = _L1_attn_setup()

    def _L1_ffn_setup():
        import jax, jax.numpy as jnp
        import numpy as np
        HIDDEN = 256
        INTER = 688
        LUT_SIZE = 16

        def _ghost_linear(x, idx, lut):
            w = lut[idx]
            return jnp.einsum('bsh,oh->bso', x, w)
        key = jax.random.key(seed)
        k_x, k_lut, k_g, k_u, k_d = jax.random.split(key, 5)
        x = jax.random.normal(k_x, (2, 512, HIDDEN), dtype=jnp.float32)
        lut = jax.random.normal(k_lut, (LUT_SIZE,), dtype=jnp.float32) * 0.02
        gate_idx = jax.random.randint(k_g, (INTER, HIDDEN), 0, LUT_SIZE, dtype=jnp.int32)
        up_idx = jax.random.randint(k_u, (INTER, HIDDEN), 0, LUT_SIZE, dtype=jnp.int32)
        down_idx = jax.random.randint(k_d, (HIDDEN, INTER), 0, LUT_SIZE, dtype=jnp.int32)
        return {'x': x, 'lut': lut, 'gate_idx': gate_idx, 'up_idx': up_idx, 'down_idx': down_idx}
    _L1_ffn_in = _L1_ffn_setup()
    _d = {'L0_attn_x': _L0_attn_in['x'], 'L0_attn_Wq': _L0_attn_in['Wq'], 'L0_attn_bq': _L0_attn_in['bq'], 'L0_attn_Wk': _L0_attn_in['Wk'], 'L0_attn_bk': _L0_attn_in['bk'], 'L0_attn_Wv': _L0_attn_in['Wv'], 'L0_attn_bv': _L0_attn_in['bv'], 'L0_attn_Wo': _L0_attn_in['Wo'], 'L0_attn_bo': _L0_attn_in['bo'], 'L0_ffn_w_router': _L0_ffn_in['w_router'], 'L0_ffn_we1': _L0_ffn_in['we1'], 'L0_ffn_we3': _L0_ffn_in['we3'], 'L0_ffn_we2': _L0_ffn_in['we2'], 'L0_ffn_ws1': _L0_ffn_in['ws1'], 'L0_ffn_ws3': _L0_ffn_in['ws3'], 'L0_ffn_ws2': _L0_ffn_in['ws2'], 'L1_attn_Wq': _L1_attn_in['Wq'], 'L1_attn_Wk': _L1_attn_in['Wk'], 'L1_attn_Wv': _L1_attn_in['Wv'], 'L1_attn_Wp': _L1_attn_in['Wp'], 'L1_ffn_lut': _L1_ffn_in['lut'], 'L1_ffn_gate_idx': _L1_ffn_in['gate_idx'], 'L1_ffn_up_idx': _L1_ffn_in['up_idx'], 'L1_ffn_down_idx': _L1_ffn_in['down_idx']}
    _x0 = _d['L0_attn_x']
    _d['L0_attn_x'] = jax.random.normal(jax.random.fold_in(jax.random.key(seed), 1), (4, 1024, 256), dtype=_x0.dtype)
    del _x0
    return _d

def reference(L0_attn_x, L0_attn_Wq, L0_attn_bq, L0_attn_Wk, L0_attn_bk, L0_attn_Wv, L0_attn_bv, L0_attn_Wo, L0_attn_bo, L0_ffn_w_router, L0_ffn_we1, L0_ffn_we3, L0_ffn_we2, L0_ffn_ws1, L0_ffn_ws3, L0_ffn_ws2, L1_attn_Wq, L1_attn_Wk, L1_attn_Wv, L1_attn_Wp, L1_ffn_lut, L1_ffn_gate_idx, L1_ffn_up_idx, L1_ffn_down_idx):

    def _L0_attn_ref(x, Wq, bq, Wk, bk, Wv, bv, Wo, bo):
        import jax, jax.numpy as jnp
        import numpy as np
        EMBED_DIM = 256
        NUM_HEADS = 16
        HEAD_DIM = EMBED_DIM // NUM_HEADS
        B, T = (4, 256)
        Bb, Tt, C = x.shape
        H, D = (NUM_HEADS, C // NUM_HEADS)
        q = (jnp.einsum('btc,oc->bto', x, Wq) + bq).reshape(Bb, Tt, H, D).transpose(0, 2, 1, 3)
        k = (jnp.einsum('btc,oc->bto', x, Wk) + bk).reshape(Bb, Tt, H, D).transpose(0, 2, 1, 3)
        v = (jnp.einsum('btc,oc->bto', x, Wv) + bv).reshape(Bb, Tt, H, D).transpose(0, 2, 1, 3)
        logits = jnp.einsum('bhqd,bhkd->bhqk', q, k) / jnp.sqrt(jnp.float32(D))
        causal = jnp.triu(jnp.ones((Tt, Tt), dtype=bool), 1)
        logits = jnp.where(causal, -jnp.inf, logits)
        attn = jax.nn.softmax(logits, axis=-1)
        out = jnp.einsum('bhqk,bhkd->bhqd', attn, v)
        out = out.transpose(0, 2, 1, 3).reshape(Bb, Tt, C)
        y = jnp.einsum('btc,oc->bto', out, Wo) + bo
        return y

    def _L0_ffn_ref(x, w_router, we1, we3, we2, ws1, ws3, ws2):
        import jax, jax.numpy as jnp
        import numpy as np
        TOP_K = 4
        B, S, D = x.shape
        T = B * S
        E = w_router.shape[1]
        xt = x.reshape(T, D)
        probs = jax.nn.softmax(xt @ w_router, axis=-1)
        top_w, top_i = jax.lax.top_k(probs, TOP_K)
        top_w = top_w / jnp.sum(top_w, axis=-1, keepdims=True)
        cw = jnp.zeros((T, E), xt.dtype).at[jnp.arange(T)[:, None], top_i].add(top_w)
        g = jax.nn.silu(jnp.einsum('td,edh->teh', xt, we1)) * jnp.einsum('td,edh->teh', xt, we3)
        g = g * cw[:, :, None]
        moe_out = jnp.einsum('teh,ehd->td', g, we2)
        shared = jax.nn.silu(xt @ ws1) * (xt @ ws3) @ ws2
        k = TOP_K
        out = shared / (k + 1) + moe_out * (k / (k + 1))
        return out.reshape(B, S, D)

    def _L1_attn_ref(x, Wq, Wk, Wv, Wp):
        import jax, jax.numpy as jnp
        import numpy as np
        import math
        NUM_HEADS = 16
        B, S, D = x.shape
        H = NUM_HEADS
        hd = D // H
        q = (x @ Wq.T).reshape(B, S, H, hd).transpose(0, 2, 1, 3)
        k = (x @ Wk.T).reshape(B, S, H, hd).transpose(0, 2, 1, 3)
        v = (x @ Wv.T).reshape(B, S, H, hd).transpose(0, 2, 1, 3)
        scores = jnp.einsum('bhqd,bhkd->bhqk', q, k) / jnp.sqrt(jnp.asarray(hd, x.dtype))
        causal = jnp.triu(jnp.ones((S, S), dtype=bool), k=1)
        scores = jnp.where(causal, -jnp.inf, scores)
        attn = jax.nn.softmax(scores, axis=-1)
        out = jnp.einsum('bhqk,bhkd->bhqd', attn, v)
        out = out.transpose(0, 2, 1, 3).reshape(B, S, D)
        return out @ Wp.T

    def _L1_ffn_ref(x, lut, gate_idx, up_idx, down_idx):
        import jax, jax.numpy as jnp
        import numpy as np
        HIDDEN = 256
        INTER = 688
        LUT_SIZE = 16

        def _ghost_linear(x, idx, lut):
            w = lut[idx]
            return jnp.einsum('bsh,oh->bso', x, w)
        gate = _ghost_linear(x, gate_idx, lut)
        up = _ghost_linear(x, up_idx, lut)
        h = jax.nn.silu(gate) * up
        return _ghost_linear(h, down_idx, lut)
    x = L0_attn_x
    x = x + 0.5 * _L0_ffn_ref(_layernorm(x, axis=-1), L0_ffn_w_router, L0_ffn_we1, L0_ffn_we3, L0_ffn_we2, L0_ffn_ws1, L0_ffn_ws3, L0_ffn_ws2)
    x = x + _L0_attn_ref(_layernorm(x, axis=-1), L0_attn_Wq, L0_attn_bq, L0_attn_Wk, L0_attn_bk, L0_attn_Wv, L0_attn_bv, L0_attn_Wo, L0_attn_bo)
    x = x + 0.5 * _L0_ffn_ref(_layernorm(x, axis=-1), L0_ffn_w_router, L0_ffn_we1, L0_ffn_we3, L0_ffn_we2, L0_ffn_ws1, L0_ffn_ws3, L0_ffn_ws2)
    x = x + 0.5 * _L1_ffn_ref(_layernorm(x, axis=-1), L1_ffn_lut, L1_ffn_gate_idx, L1_ffn_up_idx, L1_ffn_down_idx)
    x = x + _L1_attn_ref(_layernorm(x, axis=-1), L1_attn_Wq, L1_attn_Wk, L1_attn_Wv, L1_attn_Wp)
    x = x + 0.5 * _L1_ffn_ref(_layernorm(x, axis=-1), L1_ffn_lut, L1_ffn_gate_idx, L1_ffn_up_idx, L1_ffn_down_idx)
    return x

_drawn_inputs = setup_inputs


def setup_inputs(seed=0):
    import zlib

    import numpy as np

    out = dict(_drawn_inputs(seed))
    spreads = {'L0_attn_bq': (0.0, 0.497),
     'L0_attn_bk': (0.0, 0.8),
     'L0_attn_bv': (0.0, 0.1),
     'L0_attn_bo': (0.0, 0.1)}
    factors = {}
    for name, (base, spread) in spreads.items():
        noise = np.random.default_rng([zlib.crc32(name.encode()), seed]).standard_normal(out[name].shape)
        drawn = base * np.exp(spread * noise) if base else spread * noise
        out[name] = jnp.asarray(drawn.astype(out[name].dtype))
    for name, factor in factors.items():
        out[name] = (out[name] * factor).astype(out[name].dtype)
    return out
```

```python
import concourse.bass as bass
from concourse import mybir
from contextlib import ExitStack

ALU = mybir.AluOpType
ACT = mybir.ActivationFunctionType
AX = mybir.AxisListType
F32 = mybir.dt.float32
F32R = mybir.dt.float32r
BF16 = mybir.dt.bfloat16
I32 = mybir.dt.int32

P = 128
TOK = 4096
D = 256
KD = D // P
TILE = 512
SUB = TILE // P
TILES = TOK // TILE
E = 16
TOP_K = 4
EPS = 1e-5


def wait_alone(engine, sem, value, passed):
    engine.wait_ge(sem, value)
    engine.sem_inc(passed, 1)


def layer_norm_moments(dve, x, stats, moments, stats_done, moments_done, passed, n):
    for s in range(SUB):
        last = dve.bn_stats(stats[:, s, :], x[:, s, :])
    last.then_inc(stats_done, 1)
    wait_alone(dve, stats_done, n + 1, passed)
    for s in range(SUB):
        last = dve.bn_aggr(moments[:, s, :], stats[:, s, :])
    last.then_inc(moments_done, 1)


def ffn_phase(nc, name, x_in, x_out, chunks, weight_loads, gain, consts, w_router=None, background=None):
    routed = w_router is not None
    shared = chunks - (E if routed else 0)
    NC = chunks
    FRONT = 4 if routed else 2
    USES = FRONT + 2
    if routed:
        AT = {"stats": 1, "norm": 3, "x0": 5, "x1": 6, "logits": 8, "route": 9, "top": 10, "cw": 14}
    else:
        AT = {"stats": 0, "norm": 1, "x0": 2, "x1": 3, "logits": -1, "route": -1, "top": -1, "cw": -1}
    HB = 4
    EARLY = NC * 2 // 5
    ident, eps, neg_half, sel = consts["ident"], consts["eps"], consts["neg_half"], consts["sel"]

    with ExitStack() as ctx:
        def sb(n, shape, dt=F32):
            return ctx.enter_context(nc.sbuf_tensor(f"{name}_{n}", shape, dt))

        def ps(n, shape, dt=F32):
            return ctx.enter_context(nc.psum_tensor(f"{name}_{n}", shape, dt))

        def sem(n):
            return ctx.enter_context(nc.semaphore(f"{name}_{n}"))

        w_hi = sb("w_hi", [P, NC, 3 * D], F32R)
        w_lo = sb("w_lo", [P, NC, 3 * D], F32R)
        RAW = 4
        w_raw = sb("w_raw", [P, RAW, 3 * D])
        x_sb = sb("x_sb", [P, 2, SUB, D])
        xn = sb("xn", [P, SUB, D])
        stats = sb("stats", [P, SUB, 6])
        moments = sb("moments", [P, SUB, 2])
        var_eps = sb("var_eps", [P, SUB])
        rstd = sb("rstd", [P, SUB])
        xT_hi = sb("xT_hi", [P, 2, KD, TILE], F32R)
        xT_lo = sb("xT_lo", [P, 2, KD, TILE], F32R)
        gate = sb("gate", [P, 2, TILE])
        hid0 = sb("hid0", [P, TILE])
        hid = sb("hid", [P, 2, TILE])
        h_hi = sb("h_hi", [P, HB, TILE], F32R)
        h_lo = sb("h_lo", [P, HB, TILE], F32R)
        yT = sb("yT", [P, KD, TILE])
        if routed:
            wr_raw = sb("wr_raw", [P, KD, E])
            wr = sb("wr", [P, 2, KD, E], F32R)
            top_in = sb("top_in", [P, SUB, E + TOP_K])
            top_out = sb("top_out", [P, SUB, E + TOP_K])
            shifted = sb("shifted", [P, SUB, E])
            row_max = sb("row_max", [P, SUB])
            top8 = sb("top8", [P, SUB, 8])
            top_sum = sb("top_sum", [P, SUB])
            inv_sum = sb("inv_sum", [P, SUB])
            cw_raw = sb("cw_raw", [P, SUB, E])
            cw = sb("cw", [P, SUB, E])
            cw_parts = sb("cw_parts", [P, SUB, P])
            cwT = sb("cwT", [P, 2, TILE], F32R)
        g_ps = ps("g_ps", [P, 2, TILE])
        u_ps = ps("u_ps", [P, 2, TILE])
        y_ps = ps("y_ps", [P, KD, TILE])
        c_ps = ps("c_ps", [P, TILE])
        t_ps = ps("t_ps", [P, TILE])

        x_loaded = [sem("x_loaded0"), sem("x_loaded1")]
        x_stored = sem("x_stored")
        raw_loaded = [sem(f"raw_loaded{r}") for r in range(RAW)]
        w_hi_ready = sem("w_hi_ready")
        w_ready = sem("w_ready")
        early_hi_ready = sem("early_hi_ready")
        early_ready = sem("early_ready")
        stats_done = sem("stats_done")
        moments_done = sem("moments_done")
        var_done = sem("var_done")
        rstd_ready = sem("rstd_ready")
        xn_ready = sem("xn_ready")
        xh_ready = sem("xh_ready")
        passed = sem("passed")
        t_full = sem("t_full")
        t_free = sem("t_free")
        g_full = sem("g_full")
        u_full = sem("u_full")
        c_full = sem("c_full")
        gate_ready = sem("gate_ready")
        hid0_ready = sem("hid0_ready")
        hid_ready = sem("hid_ready")
        hh_ready = sem("hh_ready")
        h_ready = sem("h_ready")
        h_used = sem("h_used")
        y0_free = sem("y0_free")
        y1_free = sem("y1_free")
        sems = [x_stored, *x_loaded, *raw_loaded, w_hi_ready, w_ready, early_hi_ready, early_ready, stats_done, moments_done, var_done, rstd_ready,
                xn_ready, xh_ready, passed, t_full, t_free, g_full, u_full, c_full, gate_ready, hid0_ready,
                hid_ready, hh_ready, h_ready, h_used, y0_free, y1_free]
        if routed:
            wr_loaded = sem("wr_loaded")
            wr_hi_ready = sem("wr_hi_ready")
            wr_ready = sem("wr_ready")
            pads_ready = sem("pads_ready")
            max_ready = sem("max_ready")
            exp_ready = sem("exp_ready")
            route_step = sem("route_step")
            cw_ready = sem("cw_ready")
            sems += [wr_loaded, wr_hi_ready, wr_ready, pads_ready, max_ready, exp_ready, route_step, cw_ready]

        x_in_v = x_in.rearrange("(t s p) d -> t p s d", p=P, s=SUB)
        x_out_v = x_out.rearrange("(t s p) d -> t p s d", p=P, s=SUB)

        def wait_split(engine, c):
            if c < EARLY:
                engine.wait_ge(early_ready, c + 1)
            else:
                engine.wait_ge(w_ready, c - EARLY + 1)

        def wait_raw(engine, c):
            before = range(c % RAW, c + 1, RAW)
            engine.wait_ge(raw_loaded[c % RAW], 16 * sum(len(weight_loads(b, w_raw[:, 0, :])) for b in before))

        with nc.Block() as block:

            @block.sync
            def _(sp):
                def load(t, p):
                    sp.dma_start(x_sb[:, p, :, :], x_in_v[t, :, :, :]).then_inc(x_loaded[p], 16)

                if routed:
                    sp.dma_start(wr_raw[:, :, :], w_router.rearrange("(k p) e -> p k e", p=P)).then_inc(wr_loaded, 16)
                load(0, 0)
                load(1, 1)
                for c in range(NC):
                    if c >= RAW:
                        wait_split(sp, c - RAW)
                    for dst, src in weight_loads(c, w_raw[:, c % RAW, :]):
                        sp.dma_start(dst, src).then_inc(raw_loaded[c % RAW], 16)
                with sp.Fori(0, TILES // 2) as i:
                    for p in range(2):
                        sp.wait_ge(t_free, (2 * i + p + 1) * USES + FRONT)
                        sp.dma_start(x_out_v[2 * i + p, :, :, :], x_sb[:, p, :, :]).then_inc(x_stored, 16)
                        sp.wait_ge(x_stored, 32 * i + 16 * p + 16)
                        load((2 * i + p + 2) % TILES, p)
                sp.wait_ge(x_loaded[0], 16 * (TILES // 2 + 1))
                sp.wait_ge(x_loaded[1], 16 * (TILES // 2 + 1))

            @block.gpsimd
            def _(pool):
                def rstd_of(n):
                    pool.wait_ge(moments_done, n + 1)
                    pool.tensor_tensor(var_eps[:, :], moments[:, :, 1], eps[:, :], ALU.add).then_inc(var_done, 1)
                    pool.wait_ge(var_done, n + 1)
                    pool.tensor_tensor(rstd[:, :], var_eps[:, :], neg_half[:, :], ALU.pow).then_inc(rstd_ready, 1)

                rstd_of(0)
                if routed:
                    pool.wait_ge(wr_loaded, 16)
                    pool.tensor_copy(wr[:, 0, :, :], wr_raw[:, :, :]).then_inc(wr_hi_ready, 1)
                    pool.wait_ge(wr_hi_ready, 1)
                    pool.tensor_tensor(wr[:, 1, :, :], wr_raw[:, :, :], wr[:, 0, :, :].bitcast(F32),
                                       ALU.subtract).then_inc(wr_ready, 1)
                for c in range(EARLY, NC):
                    wait_raw(pool, c)
                    pool.tensor_copy(w_hi[:, c, :], w_raw[:, c % RAW, :]).then_inc(w_hi_ready, 1)
                    pool.wait_ge(w_hi_ready, c - EARLY + 1)
                    pool.tensor_tensor(w_lo[:, c, :], w_raw[:, c % RAW, :], w_hi[:, c, :].bitcast(F32),
                                       ALU.subtract).then_inc(w_ready, 1)
                    if c == EARLY:
                        rstd_of(1)
                with pool.Fori(2, TILES + 1) as n:
                    rstd_of(n)

            def front_steps(step):
                return [k for k, at in AT.items() if at == step]

            @block.tensor
            def _(pe):
                def split_mms(out, pairs, start, stop):
                    for n, (a, b) in enumerate(pairs):
                        last = pe.matmul(out, a, b, start=(start and n == 0), stop=(stop and n == len(pairs) - 1))
                    return last

                def use_bank(use):
                    pe.wait_ge(t_free, use)

                def x_turn(n, use, kd):
                    pe.wait_ge(xn_ready, n + 1)
                    for s in range(SUB):
                        last = pe.transpose(t_ps[:, s * P:(s + 1) * P], xn[:, s, kd * P:(kd + 1) * P], ident[:, :])
                    last.then_inc(t_full, 1)

                def logits(q, use):
                    for s in range(SUB):
                        pairs = []
                        for kd in range(KD):
                            for a, b in ((xT_hi, 0), (xT_hi, 1), (xT_lo, 0), (xT_lo, 1)):
                                pairs.append((a[:, q, kd, s * P:(s + 1) * P], wr[:, b, kd, :]))
                        last = split_mms(t_ps[:, s * E:(s + 1) * E], pairs, True, True)
                    last.then_inc(t_full, 1)

                def cw_turn(n):
                    pe.wait_ge(cw_ready, n + 1)
                    for s in range(SUB):
                        last = pe.transpose(t_ps[:, s * P:(s + 1) * P], cw_parts[:, s, :], ident[:, :])
                    last.then_inc(t_full, 1)

                def front(n, q, use, steps):
                    for k in steps:
                        if k == "x0":
                            if not isinstance(use, int) or use > 0:
                                use_bank(use)
                            x_turn(n, use, 0)
                        if k == "x1":
                            use_bank(use + 1)
                            x_turn(n, use + 1, 1)
                        if k == "logits" and routed:
                            use_bank(use + 2)
                            logits(q, use + 2)
                        if k == "cw" and routed:
                            use_bank(use + 3)
                            cw_turn(n)

                def gate_up(g, q, c):
                    b = c % 2
                    wait_split(pe, c)
                    pe.wait_ge(hid_ready, g + 1)
                    for ps_, off, full in ((g_ps, 0, g_full), (u_ps, D, u_full)):
                        pairs = []
                        for kd in range(KD):
                            cols = slice(off + kd * P, off + (kd + 1) * P)
                            pairs += [(w_hi[:, c, cols], xT_hi[:, q, kd, :]), (w_hi[:, c, cols], xT_lo[:, q, kd, :]),
                                      (w_lo[:, c, cols], xT_hi[:, q, kd, :])]
                        split_mms(ps_[:, b, :], pairs, True, True).then_inc(full, 1)

                def spread_weight(g, q, c):
                    pe.wait_ge(hid_ready, g + 2)
                    pe.matmul(c_ps[:, :], sel[:, (c - shared) * P:(c - shared + 1) * P], cwT[:, q, :],
                              start=True, stop=True).then_inc(c_full, 1)

                def down(g, c):
                    b = c % HB
                    pe.wait_ge(h_ready, g + 3)
                    for m in range(KD):
                        cols = slice(2 * D + m * P, 2 * D + (m + 1) * P)
                        last = split_mms(y_ps[:, m, :], [(w_hi[:, c, cols], h_hi[:, b, :]), (w_hi[:, c, cols], h_lo[:, b, :]),
                                                         (w_lo[:, c, cols], h_hi[:, b, :])], c == 0, c == NC - 1)
                    last.then_inc(h_used, 1)

                pe.sem_inc(h_used, HB)
                if routed:
                    pe.wait_ge(wr_ready, 1)
                front(0, 0, 0, list(AT))
                with pe.Fori(0, TILES // 2) as i:
                    for q in range(2):
                        t = 2 * i + q
                        use = t * USES + FRONT
                        pe.wait_ge(t_free, use)
                        for c in range(NC):
                            gate_up(t * NC + c, q, c)
                            if c >= shared:
                                spread_weight(t * NC + c, q, c)
                            if c == 2:
                                pe.wait_ge(y0_free, t + 1)
                                pe.wait_ge(y1_free, t + 1)
                            if c >= 2:
                                down(t * NC + c - 2, c - 2)
                            front(t + 1, 1 - q, use, front_steps(c))
                        down(t * NC + NC - 2, NC - 2)
                        down(t * NC + NC - 1, NC - 1)
                        for half in range(2):
                            use_bank(use + FRONT + half)
                            pe.wait_ge(y0_free, t + 2)
                            pe.wait_ge(y1_free, t + 2)
                            for s in range(2):
                                for m in range(KD):
                                    last = pe.transpose(t_ps[:, s * D + m * P:s * D + (m + 1) * P],
                                                        yT[:, m, (2 * half + s) * P:(2 * half + s + 1) * P], ident[:, :])
                            last.then_inc(t_full, 1)

            @block.scalar
            def _(act):
                def front(n, q, use, steps):
                    for k in steps:
                        if k in ("x0", "x1"):
                            kd = int(k[1])
                            act.wait_ge(t_full, use + kd + 1)
                            act.activation(xT_hi[:, q, kd, :], t_ps[:, :], ACT.Copy).then_inc(xh_ready, 1)
                        if k == "route" and routed:
                            act.wait_ge(t_free, use + 3)
                            act.activation(top_in[:, :, 0:E], shifted[:, :, :], ACT.Exp).then_inc(exp_ready, 1)
                        if k == "cw" and routed:
                            act.wait_ge(t_full, use + 4)
                            act.activation(cwT[:, q, :], t_ps[:, :], ACT.Copy).then_inc(t_free, 1)

                def hidden_hi(g, c):
                    act.wait_ge(hid_ready, g + 3)
                    act.wait_ge(h_used, g + 1)
                    act.activation(h_hi[:, c % HB, :], hid[:, c % 2, :], ACT.Copy).then_inc(hh_ready, 1)

                act.sem_inc(y0_free, 1)
                for c in range(EARLY):
                    wait_raw(act, c)
                    act.activation(w_hi[:, c, :], w_raw[:, c % RAW, :], ACT.Copy).then_inc(early_hi_ready, 1)
                    if c == 1:
                        front(0, 0, 0, list(AT))
                with act.Fori(0, TILES // 2) as i:
                    for q in range(2):
                        t = 2 * i + q
                        use = t * USES + FRONT
                        for c in range(NC):
                            g = t * NC + c
                            act.wait_ge(g_full, g + 1)
                            act.activation(gate[:, c % 2, :], g_ps[:, c % 2, :], ACT.Silu).then_inc(gate_ready, 1)
                            if c >= 1:
                                hidden_hi(g - 1, c - 1)
                            front(t + 1, 1 - q, use, front_steps(c))
                        hidden_hi(t * NC + NC - 1, NC - 1)
                        act.wait_ge(h_used, HB + (t + 1) * NC)
                        act.activation(yT[:, 0, :], y_ps[:, 0, :], ACT.Copy).then_inc(y0_free, 1)

            @block.vector
            def _(dve):
                def front(n, q, use, steps, n_q=None):
                    for k in steps:
                        if k == "stats":
                            dve.wait_ge(x_loaded[q], 16 * n_q)
                            layer_norm_moments(dve, x_sb[:, q, :, :], stats, moments, stats_done, moments_done, passed, n)
                        if k == "norm":
                            dve.wait_ge(rstd_ready, n + 1)
                            for s in range(SUB):
                                last = dve.tensor_scalar(xn[:, s, :], x_sb[:, q, s, :], moments[:, s, 0:1], rstd[:, s:s + 1],
                                                         ALU.subtract, ALU.mult)
                            last.then_inc(xn_ready, 1)
                        if k in ("x0", "x1"):
                            kd = int(k[1])
                            dve.wait_ge(xh_ready, 2 * n + kd + 1)
                            dve.tensor_tensor(xT_lo[:, q, kd, :], t_ps[:, :], xT_hi[:, q, kd, :].bitcast(F32),
                                              ALU.subtract).then_inc(t_free, 1)
                        if k == "route" and routed:
                            logit = t_ps[:, 0:SUB * E].rearrange("p (s e) -> p s e", e=E)
                            dve.wait_ge(t_full, use + 3)
                            dve.tensor_reduce(row_max[:, :], logit, AX.X, ALU.max).then_inc(max_ready, 1)
                            dve.wait_ge(max_ready, n + 1)
                            dve.tensor_tensor(shifted[:, :, :], logit, row_max[:, :].unsqueeze(2).to_broadcast([P, SUB, E]),
                                              ALU.subtract).then_inc(t_free, 1)
                        if k == "top" and routed:
                            wait_alone(dve, exp_ready, n + 1, passed)
                            for s in range(SUB):
                                last = dve.max(top8[:, s, :], top_in[:, s, :])
                            last.then_inc(route_step, 1)
                            dve.wait_ge(route_step, n * 7 + 1)
                            dve.tensor_reduce(top_sum[:, :], top8[:, :, 0:TOP_K], AX.X, ALU.add).then_inc(route_step, 1)
                            dve.memset(top8[:, :, TOP_K:8], -1.0).then_inc(route_step, 1)
                            dve.wait_ge(route_step, n * 7 + 3)
                            dve.reciprocal(inv_sum[:, :], top_sum[:, :])
                            for s in range(SUB):
                                last = dve.match_replace(top_out[:, s, :], top8[:, s, :], top_in[:, s, :], 0.0)
                            last.then_inc(route_step, 1)
                            dve.wait_ge(route_step, n * 7 + 4)
                            dve.tensor_tensor(cw_raw[:, :, :], top_in[:, :, 0:E], top_out[:, :, 0:E], ALU.subtract)\
                               .then_inc(route_step, 1)
                            dve.wait_ge(route_step, n * 7 + 5)
                            for s in range(SUB):
                                last = dve.tensor_scalar(cw[:, s, :], cw_raw[:, s, :], inv_sum[:, s:s + 1], gain["routed"],
                                                         ALU.mult, ALU.mult)
                            last.then_inc(route_step, 1)
                            dve.wait_ge(route_step, n * 7 + 6)
                            dve.tensor_copy(cw_parts[:, :, 0:E].bitcast(F32R), cw[:, :, :]).then_inc(route_step, 1)
                            dve.wait_ge(route_step, n * 7 + 7)
                            dve.tensor_tensor(cw_parts[:, :, E:2 * E], cw[:, :, :], cw_parts[:, :, 0:E], ALU.subtract)\
                               .then_inc(cw_ready, 1)

                def product(g, c, t):
                    b = c % 2
                    dve.wait_ge(gate_ready, g + 1)
                    dve.wait_ge(u_full, g + 1)
                    dve.wait_ge(h_ready, g + 1)
                    if c < shared:
                        dve.scalar_tensor_tensor(out=hid[:, b, :], in0=gate[:, b, :], scalar=gain["shared"], in1=u_ps[:, b, :],
                                                 op0=ALU.mult, op1=ALU.mult).then_inc(hid_ready, 1)
                    else:
                        n = t * E + (c - shared) + 1
                        dve.wait_ge(hid_ready, g + 2)
                        dve.tensor_tensor(hid0[:, :], gate[:, b, :], u_ps[:, b, :], ALU.mult).then_inc(hid0_ready, 1)
                        dve.wait_ge(hid0_ready, n)
                        dve.wait_ge(c_full, n)
                        dve.tensor_tensor(hid[:, b, :], hid0[:, :], c_ps[:, :], ALU.mult).then_inc(hid_ready, 1)

                def hidden_lo(g, c):
                    dve.wait_ge(hh_ready, g + 1)
                    dve.tensor_tensor(h_lo[:, c % HB, :], hid[:, c % 2, :], h_hi[:, c % HB, :].bitcast(F32),
                                      ALU.subtract).then_inc(h_ready, 1)

                dve.sem_inc(hid_ready, 2)
                dve.sem_inc(h_ready, 2)
                dve.sem_inc(y1_free, 1)
                if routed:
                    dve.memset(cw_parts[:, :, :], 0.0).then_inc(pads_ready, 1)
                    dve.memset(top_in[:, :, E:], -1.0).then_inc(pads_ready, 1)
                    dve.wait_ge(pads_ready, 2)
                for c in range(EARLY):
                    dve.wait_ge(early_hi_ready, c + 1)
                    dve.tensor_tensor(w_lo[:, c, :], w_raw[:, c % RAW, :], w_hi[:, c, :].bitcast(F32), ALU.subtract)\
                        .then_inc(early_ready, 1)
                    if c == 1:
                        front(0, 0, 0, list(AT), 1)
                with dve.Fori(0, TILES // 2) as i:
                    for q in range(2):
                        t = 2 * i + q
                        use = t * USES + FRONT
                        for c in range(NC):
                            g = t * NC + c
                            product(g, c, t)
                            if c >= 1:
                                hidden_lo(g - 1, c - 1)
                            front(t + 1, 1 - q, use, front_steps(c), i + 1 + (1 if q == 1 else 0))
                        hidden_lo(t * NC + NC - 1, NC - 1)
                        dve.wait_ge(h_used, HB + (t + 1) * NC)
                        dve.tensor_copy(yT[:, 1, :], y_ps[:, 1, :]).then_inc(y1_free, 1)
                        for half in range(2):
                            dve.wait_ge(t_full, use + FRONT + half + 1)
                            xs = x_sb[:, q, 2 * half:2 * half + 2, :]
                            dve.tensor_tensor(xs, xs, t_ps[:, :].rearrange("p (s d) -> p s d", d=D), ALU.add)\
                               .then_inc(t_free, 1)

        with nc.Block() as block:
            @block.sync
            def _(sp):
                for s in sems:
                    sp.sem_clear(s)


HEADS = 16
HD = D // HEADS
SEQ = 1024
BATCH = TOK // SEQ
QT = SEQ // P
VW = HD + 1
BIG = -1e30


def project_phase(nc, name, x_in, w_qkv, b_qkv, q_dram, k_dram, v_sb, consts):
    ident, eps, neg_half = consts["ident"], consts["eps"], consts["neg_half"]
    biased = b_qkv is not None
    USES = KD
    with ExitStack() as ctx:
        def sb(n, shape, dt=F32):
            return ctx.enter_context(nc.sbuf_tensor(f"{name}_{n}", shape, dt))

        def ps(n, shape, dt=F32):
            return ctx.enter_context(nc.psum_tensor(f"{name}_{n}", shape, dt))

        sems = []

        def sem(n):
            sems.append(ctx.enter_context(nc.semaphore(f"{name}_{n}")))
            return sems[-1]

        w_raw = sb("w_raw", [P, 3, KD, D])
        w_hi = sb("w_hi", [P, 3, KD, D], F32R)
        w_lo = sb("w_lo", [P, 3, KD, D], F32R)
        x_sb = sb("x_sb", [P, 2, SUB, D])
        xn = sb("xn", [P, SUB, D])
        stats = sb("stats", [P, SUB, 6])
        moments = sb("moments", [P, SUB, 2])
        var_eps = sb("var_eps", [P, SUB])
        rstd = sb("rstd", [P, SUB])
        xT_hi = sb("xT_hi", [P, 2, KD, TILE], F32R)
        xT_lo = sb("xT_lo", [P, 2, KD, TILE], F32R)
        qk_hi = sb("qk_hi", [P, 2, 4, TILE], F32R)
        qk_lo = sb("qk_lo", [P, 2, 4, TILE], F32R)
        if biased:
            b_col = sb("b_col", [P, 4])
            bv_row = sb("bv_row", [P, D])
        t_ps = ps("t_ps", [P, TILE])
        qk_ps = ps("qk_ps", [P, 4, TILE])
        v_ps = ps("v_ps", [P, 2, 2, D])

        x_loaded = [sem("x_loaded0"), sem("x_loaded1")]
        w_loaded = sem("w_loaded")
        passed = sem("passed")
        b_loaded = sem("b_loaded")
        w_hi_ready = sem("w_hi_ready")
        w_ready = sem("w_ready")
        ones_ready = sem("ones_ready")
        stats_done = sem("stats_done")
        moments_done = sem("moments_done")
        var_done = sem("var_done")
        rstd_ready = sem("rstd_ready")
        xn_ready = sem("xn_ready")
        xh_ready = sem("xh_ready")
        t_full = sem("t_full")
        t_free = sem("t_free")
        qk_full = sem("qk_full")
        qk_hi_ready = sem("qk_hi_ready")
        qk_ready = sem("qk_ready")
        qk_stored = [sem("qk_stored0"), sem("qk_stored1")]
        v_full = sem("v_full")
        v_ready = sem("v_ready")

        x_in_v = x_in.rearrange("(t s p) d -> t p s d", p=P, s=SUB)
        v_v = v_sb[:, :].rearrange("p (b h k w) -> p b h k w", b=BATCH, h=HEADS, k=QT)

        with nc.Block() as block:

            @block.sync
            def _(sp):
                def load(t, p):
                    sp.dma_start(x_sb[:, p, :, :], x_in_v[t, :, :, :]).then_inc(x_loaded[p], 16)

                for p in range(2):
                    sp.sem_inc(qk_stored[p], 128)
                load(0, 0)
                for n, w in enumerate(w_qkv):
                    sp.dma_start(w_raw[:, n, :, :], w.rearrange("(k p) o -> p k o", p=P)).then_inc(w_loaded, 16)
                load(1, 1)
                if biased:
                    for n in range(2):
                        sp.dma_start(b_col[:, 2 * n:2 * n + 2], b_qkv[n].rearrange("(m p) -> p m", p=P),
                                     allow_slow_non_contiguous=True)\
                            .then_inc(b_loaded, 16)
                    sp.dma_start(bv_row[:, :], b_qkv[2].rearrange("(a d) -> a d", a=1).to_broadcast([P, D]))\
                        .then_inc(b_loaded, 16)
                with sp.Fori(0, TILES // 2) as i:
                    for p in range(2):
                        t = 2 * i + p
                        for m in range(4):
                            dram = (q_dram, k_dram)[m // 2]
                            heads = slice((m % 2) * 8, (m % 2) * 8 + 8)
                            sp.wait_ge(qk_ready, t * 4 + m + 5)
                            for l, part in enumerate((qk_hi, qk_lo)):
                                sp.dma_start(dram[i, heads, l, :, p * TILE:(p + 1) * TILE],
                                             part[:, p, m, :].bitcast(F32)).then_inc(qk_stored[p], 16)
                        sp.wait_ge(xn_ready, t + 1)
                        load((t + 2) % TILES, p)
                for p in range(2):
                    sp.wait_ge(x_loaded[p], 16 * (TILES // 2 + 1))
                    sp.wait_ge(qk_stored[p], 128 * (TILES // 2 + 1))

            @block.gpsimd
            def _(pool):
                def rstd_of(n):
                    pool.wait_ge(moments_done, n + 1)
                    pool.tensor_tensor(var_eps[:, :], moments[:, :, 1], eps[:, :], ALU.add).then_inc(var_done, 1)
                    pool.wait_ge(var_done, n + 1)
                    pool.tensor_tensor(rstd[:, :], var_eps[:, :], neg_half[:, :], ALU.pow).then_inc(rstd_ready, 1)

                rstd_of(0)
                pool.memset(v_sb[:, :].rearrange("p (n w) -> p n w", w=VW)[:, :, HD], 1.0).then_inc(ones_ready, 1)
                with pool.Fori(1, TILES + 1) as n:
                    rstd_of(n)

            @block.tensor
            def _(pe):
                def split_mms(out, pairs):
                    for n, (a, b) in enumerate(pairs):
                        last = pe.matmul(out, a, b, start=(n == 0), stop=(n == len(pairs) - 1))
                    return last

                def x_turn(n, use, kd):
                    if kd == 0:
                        pe.wait_ge(xn_ready, n + 1)
                    if not isinstance(use, int) or use + kd > 0:
                        pe.wait_ge(t_free, use + kd)
                    for s in range(SUB):
                        last = pe.transpose(t_ps[:, s * P:(s + 1) * P], xn[:, s, kd * P:(kd + 1) * P], ident[:, :])
                    last.then_inc(t_full, 1)

                x_turn(0, 0, 0)
                x_turn(0, 0, 1)
                pe.wait_ge(w_ready, 3)
                with pe.Fori(0, TILES // 2) as i:
                    for q in range(2):
                        t = 2 * i + q
                        use = (t + 1) * USES
                        pe.wait_ge(t_free, use)
                        for m in range(4):
                            pe.wait_ge(qk_ready, t * 4 + m + 1)
                            n, cols = m // 2, slice((m % 2) * P, (m % 2 + 1) * P)
                            pairs = []
                            for kd in range(KD):
                                pairs += [(w_hi[:, n, kd, cols], xT_hi[:, q, kd, :]), (w_hi[:, n, kd, cols], xT_lo[:, q, kd, :]),
                                          (w_lo[:, n, kd, cols], xT_hi[:, q, kd, :])]
                            split_mms(qk_ps[:, m, :], pairs).then_inc(qk_full, 1)
                            if m >= 2:
                                x_turn(t + 1, use, m - 2)
                        for half in range(2):
                            pe.wait_ge(v_ready, t * 2 + half + 1)
                            for s in range(2):
                                toks = slice((2 * half + s) * P, (2 * half + s + 1) * P)
                                pairs = []
                                for kd in range(KD):
                                    pairs += [(xT_hi[:, q, kd, toks], w_hi[:, 2, kd, :]), (xT_hi[:, q, kd, toks], w_lo[:, 2, kd, :]),
                                              (xT_lo[:, q, kd, toks], w_hi[:, 2, kd, :])]
                                last = split_mms(v_ps[:, half, s, :], pairs)
                            last.then_inc(v_full, 1)

            @block.scalar
            def _(act):
                def x_hi(n, q, use, kd):
                    act.wait_ge(t_full, use + kd + 1)
                    act.activation(xT_hi[:, q, kd, :], t_ps[:, :], ACT.Copy).then_inc(xh_ready, 1)

                for n in range(3):
                    act.wait_ge(w_loaded, 48)
                    act.activation(w_hi[:, n, :, :], w_raw[:, n, :, :], ACT.Copy).then_inc(w_hi_ready, 1)
                x_hi(0, 0, 0, 0)
                x_hi(0, 0, 0, 1)
                if biased:
                    act.wait_ge(b_loaded, 48)
                with act.Fori(0, TILES // 2) as i:
                    for q in range(2):
                        t = 2 * i + q
                        for m in range(4):
                            act.wait_ge(qk_full, t * 4 + m + 1)
                            act.wait_ge(qk_stored[q], i * 128 + 128)
                            if biased:
                                act.activation(qk_hi[:, q, m, :], qk_ps[:, m, :], ACT.Identity, bias=b_col[:, m:m + 1])\
                                    .then_inc(qk_hi_ready, 1)
                            else:
                                act.activation(qk_hi[:, q, m, :], qk_ps[:, m, :], ACT.Copy).then_inc(qk_hi_ready, 1)
                            if m >= 2:
                                x_hi(t + 1, 1 - q, (t + 1) * USES, m - 2)

            @block.vector
            def _(dve):
                def normalise(n, q, n_q):
                    dve.wait_ge(x_loaded[q], 16 * n_q)
                    layer_norm_moments(dve, x_sb[:, q, :, :], stats, moments, stats_done, moments_done, passed, n)
                    dve.wait_ge(rstd_ready, n + 1)
                    for s in range(SUB):
                        last = dve.tensor_scalar(xn[:, s, :], x_sb[:, q, s, :], moments[:, s, 0:1], rstd[:, s:s + 1],
                                                 ALU.subtract, ALU.mult)
                    last.then_inc(xn_ready, 1)

                def x_lo(n, q, kd):
                    dve.wait_ge(xh_ready, 2 * n + kd + 1)
                    dve.tensor_tensor(xT_lo[:, q, kd, :], t_ps[:, :], xT_hi[:, q, kd, :].bitcast(F32),
                                      ALU.subtract).then_inc(t_free, 1)

                dve.sem_inc(v_ready, 2)
                dve.sem_inc(qk_ready, 4)
                normalise(0, 0, 1)
                for n in range(3):
                    dve.wait_ge(w_hi_ready, n + 1)
                    dve.tensor_tensor(w_lo[:, n, :, :], w_raw[:, n, :, :], w_hi[:, n, :, :].bitcast(F32), ALU.subtract)\
                        .then_inc(w_ready, 1)
                x_lo(0, 0, 0)
                x_lo(0, 0, 1)
                if biased:
                    dve.wait_ge(b_loaded, 48)
                with dve.Fori(0, TILES // 2) as i:
                    for q in range(2):
                        t = 2 * i + q
                        normalise(t + 1, 1 - q, i + 1 + q)
                        for m in range(4):
                            dve.wait_ge(qk_hi_ready, t * 4 + m + 1)
                            hi = qk_hi[:, q, m, :].bitcast(F32)
                            if biased:
                                dve.scalar_tensor_tensor(out=qk_lo[:, q, m, :], in0=qk_ps[:, m, :], scalar=b_col[:, m:m + 1],
                                                         in1=hi, op0=ALU.add, op1=ALU.subtract).then_inc(qk_ready, 1)
                            else:
                                dve.tensor_tensor(qk_lo[:, q, m, :], qk_ps[:, m, :], hi, ALU.subtract).then_inc(qk_ready, 1)
                            if m >= 2:
                                x_lo(t + 1, 1 - q, m - 2)
                        for half in range(2):
                            dve.wait_ge(v_full, t * 2 + half + 1)
                            for s in range(2):
                                src = v_ps[:, half, s, :].rearrange("p (h d) -> p h d", h=HEADS)
                                dst = v_v[:, i, :, q * SUB + 2 * half + s, 0:HD]
                                if biased:
                                    last = dve.tensor_tensor(dst, src, bv_row[:, :].rearrange("p (h d) -> p h d", h=HEADS), ALU.add)
                                else:
                                    last = dve.tensor_copy(dst, src)
                            last.then_inc(v_ready, 1)

        with nc.Block() as block:
            @block.sync
            def _(sp):
                for s in sems:
                    sp.sem_clear(s)


def piece_list(width):
    return [(a, min(TILE, width - a)) for a in range(0, width, TILE)]


def heads_phase(nc, name, q_dram, k_dram, v_sb, o_sb, consts):
    identb, maskb, ident = consts["identb"], consts["maskb"], consts["ident"]
    R = 4
    N = BATCH * HEADS
    ROWS = 4 * HD
    OFF = [sum(SEQ - k * P for k in range(j)) for j in range(QT + 1)]
    PIECES = [piece_list(SEQ - j * P) for j in range(QT)]
    FIRST = [sum(len(PIECES[k]) for k in range(j)) for j in range(QT + 1)]
    NP = FIRST[QT]
    NB = 3
    assert NP % NB == 0
    HALF = TILE // P
    S_USES = [(i, a, w) for i in reversed(range(QT)) for a, w in piece_list((i + 1) * P)]
    NS = len(S_USES)
    assert NS % 2 == 0
    LOAD = 5 * 16
    with ExitStack() as ctx:
        def sb(n, shape, dt=F32):
            return ctx.enter_context(nc.sbuf_tensor(f"{name}_{n}", shape, dt))

        def ps(n, shape, dt=F32):
            return ctx.enter_context(nc.psum_tensor(f"{name}_{n}", shape, dt))

        sems = []

        def sem(n):
            sems.append(ctx.enter_context(nc.semaphore(f"{name}_{n}")))
            return sems[-1]

        q_st = sb("q_st", [P, R, SEQ], F32R)
        k_st = sb("k_st", [P, R, SEQ], F32R)
        row_max = sb("row_max", [P, 2, P])
        neg_hi = sb("neg_hi", [QT, R, P], F32R)
        neg_lo = sb("neg_lo", [QT, R, P], F32R)
        probs = sb("probs", [P, 2, OFF[QT]])
        inv_sum = sb("inv_sum", [P, 2, QT])
        s_ps = ps("s_ps", [P, 2, TILE])
        st_ps = ps("st_ps", [P, NB, TILE])
        o_banks = ps("o_ps", [P, 2, TILE])
        m_ps = ps("m_ps", [P, P])

        def o_ps(r):
            return o_banks[:, r % 2, 0:QT * VW].rearrange("p (q w) -> p q w", w=VW)

        stack_loaded = [sem(f"stack_loaded{r}") for r in range(R)]
        neg_loaded = [sem(f"neg_loaded{r}") for r in range(R)]
        ones_ready = sem("ones_ready")
        zeros_ready = sem("zeros_ready")
        s_full = sem("s_full")
        s_free = sem("s_free")
        max_ready = sem("max_ready")
        m_full = sem("m_full")
        neg_hi_ready = sem("neg_hi_ready")
        neg_ready = sem("neg_ready")
        st_full = sem("st_full")
        exp_done = sem("exp_done")
        masked = sem("masked")
        passed = sem("passed")
        pv_done = sem("pv_done")
        sum_ready = sem("sum_ready")
        o_free = sem("o_free")

        with nc.Block() as block:

            @block.sync
            def _(sp):
                def load(n, r):
                    q_v = q_dram[n, :, :, :].rearrange("l d t -> (l d) t")
                    k_v = k_dram[n, :, :, :].rearrange("l d t -> (l d) t")
                    for to, src in ((q_st[0:32, r, :], q_v), (q_st[32:64, r, :], q_v), (k_st[0:32, r, :], k_v),
                                    (k_st[32:48, r, :], k_v[HD:2 * HD, :]), (k_st[48:64, r, :], k_v[0:HD, :])):
                        sp.dma_start(to.bitcast(F32), src).then_inc(stack_loaded[r], 16)

                def put_neg(n, r):
                    sp.wait_ge(neg_ready, n + 1)
                    for row, part in ((ROWS, neg_hi), (ROWS + 1, neg_lo)):
                        sp.dma_start(q_st[row:row + 1, r, :].bitcast(F32), part[:, r, :].bitcast(F32)).then_inc(neg_loaded[r], 16)

                load(0, 0)
                load(1, 1)
                load(2, 2)
                put_neg(0, 0)
                with sp.Fori(0, N // R) as g:
                    for r in range(R):
                        n = g * R + r
                        sp.wait_ge(exp_done, n * NP + NB)
                        load((n + 3) % N, (r + 3) % R)
                        put_neg(n + 1, (r + 1) % R)
                for r in range(R):
                    sp.wait_ge(stack_loaded[r], LOAD * (N // R + (1 if r < 3 else 0)))
                    sp.wait_ge(neg_loaded[r], 32 * (N // R + (1 if r < 1 else 0)))

            @block.gpsimd
            def _(pool):
                pool.memset(k_st[ROWS:ROWS + 2, :, :].bitcast(F32), 1.0).then_inc(ones_ready, 1)
                with pool.Fori(0, N // R) as g:
                    for r in range(R):
                        n = g * R + r
                        for j in range(QT):
                            wait_alone(pool, exp_done, n * NP + FIRST[j] + 1 + NB, passed)
                            d = probs[:, r % 2, OFF[j]:OFF[j] + P]
                            pool.affine_select(out=d, in_=d, compare_op=ALU.is_ge, fill=0.0, base=0, pattern=[[1, P]],
                                               channel_multiplier=-1).then_inc(masked, 1)

            @block.tensor
            def _(pe):
                def scores(n, r, i):
                    for k, (block, a, w) in enumerate(S_USES):
                        if block != i:
                            continue
                        pe.wait_ge(s_free, n * NS + k + 1)
                        diag = a + w == (i + 1) * P
                        last = pe.matmul(s_ps[:, k % 2, 0:w], q_st[0:ROWS, r, i * P:(i + 1) * P], k_st[0:ROWS, r, a:a + w],
                                         start=True, stop=not diag)
                        if diag:
                            last = pe.matmul(s_ps[:, k % 2, w - P:w], identb[:, :], maskb[:, :], start=False, stop=True)
                        last.then_inc(s_full, 1)

                def max_turn(n, r):
                    pe.wait_ge(max_ready, n + 1)
                    if not isinstance(n, int):
                        pe.wait_ge(neg_ready, n)
                    pe.transpose(m_ps[:, :], row_max[:, r % 2, :], ident[:, :]).then_inc(m_full, 1)

                def scores_t(n, r, j):
                    for k, (a, w) in enumerate(PIECES[j]):
                        u = FIRST[j] + k
                        pe.wait_ge(exp_done, n * NP + u + 1)
                        last = pe.matmul(st_ps[:, u % NB, 0:w], k_st[0:ROWS + 2, r, j * P:(j + 1) * P],
                                         q_st[0:ROWS + 2, r, j * P + a:j * P + a + w], start=True, stop=True)
                        last.then_inc(st_full, 1)

                def times_v(n, r, i):
                    pe.wait_ge(exp_done, n * NP + FIRST[i + 1] + NB)
                    pe.wait_ge(masked, n * QT + i + 1)
                    if i == 0:
                        pe.wait_ge(o_free, n + 1)
                    for j in range(i + 1):
                        at = OFF[j] + (i - j) * P
                        last = pe.matmul(o_ps(r)[:, i, :], probs[:, r % 2, at:at + P], v_sb[:, bass.ds((n * QT + j) * VW, VW)],
                                         start=(j == 0), stop=(j == i))
                    if i == QT - 1:
                        last.then_inc(pv_done, 1)

                pe.sem_inc(pv_done, 2)
                pe.wait_ge(ones_ready, 1)
                pe.wait_ge(zeros_ready, 1)
                for n in range(2):
                    pe.wait_ge(stack_loaded[n], LOAD)
                    for i in reversed(range(QT)):
                        scores(n, n, i)
                    if n == 0:
                        max_turn(0, 0)
                with pe.Fori(0, N // R) as g:
                    for r in range(R):
                        n = g * R + r
                        r2 = (r + 2) % R
                        pe.wait_ge(stack_loaded[r2], LOAD * (g + 1 + (r + 2) // R))
                        pe.wait_ge(neg_loaded[r], 32 * (g + 1))
                        for j in range(QT):
                            scores_t(n, r, j)
                            scores(n + 2, r2, QT - 1 - j)
                            if r > 0:
                                times_v(n - 1, r - 1, j)
                            if j == 1:
                                max_turn(n + 1, (r + 1) % R)
                    for j in range(QT):
                        times_v(n, R - 1, j)

            @block.scalar
            def _(act):
                act.sem_inc(exp_done, NB)
                with act.Fori(0, N // R) as g:
                    for r in range(R):
                        n = g * R + r
                        act.wait_ge(pv_done, n + 1)
                        for j in range(QT):
                            for k, (a, w) in enumerate(PIECES[j]):
                                u = FIRST[j] + k
                                act.wait_ge(st_full, n * NP + u + 1)
                                act.activation(probs[:, r % 2, OFF[j] + a:OFF[j] + a + w], st_ps[:, u % NB, 0:w], ACT.Exp,
                                               scale=float(HD) ** -0.5).then_inc(exp_done, 1)

            @block.vector
            def _(dve):
                def reduce(n, r, i):
                    for k, (block, a, w) in enumerate(S_USES):
                        if block != i:
                            continue
                        dve.wait_ge(s_full, n * NS + k + 1)
                        col = i if a == 0 else QT + i - HALF
                        dve.tensor_reduce(row_max[:, r % 2, col:col + 1], s_ps[:, k % 2, 0:w], AX.X, ALU.max).then_inc(s_free, 1)
                    if i == 0:
                        dve.wait_ge(s_free, (n + 1) * NS + 2)
                        dve.tensor_tensor(row_max[:, r % 2, HALF:QT], row_max[:, r % 2, HALF:QT], row_max[:, r % 2, QT:QT + HALF],
                                          ALU.max).then_inc(max_ready, 1)

                def negate(n, r):
                    dve.wait_ge(m_full, n + 1)
                    dve.tensor_scalar(neg_hi[:, r, :], m_ps[0:QT, :], -1.0, None, ALU.mult).then_inc(neg_hi_ready, 1)
                    dve.wait_ge(neg_hi_ready, n + 1)
                    dve.scalar_tensor_tensor(out=neg_lo[:, r, :], in0=m_ps[0:QT, :], scalar=-1.0,
                                             in1=neg_hi[:, r, :].bitcast(F32), op0=ALU.mult, op1=ALU.subtract)\
                        .then_inc(neg_ready, 1)

                def output(n, r):
                    dve.wait_ge(pv_done, n + 3)
                    dve.wait_ge(o_free, n + 1)
                    dve.reciprocal(inv_sum[:, r % 2, :], o_ps(r)[:, :, HD]).then_inc(sum_ready, 1)
                    dve.wait_ge(sum_ready, n + 1)
                    dve.tensor_tensor(o_sb[:, bass.ds(n * QT * HD, QT * HD)].rearrange("p (q d) -> p q d", d=HD),
                                      o_ps(r)[:, :, 0:HD], inv_sum[:, r % 2, :].unsqueeze(2).to_broadcast([P, QT, HD]), ALU.mult)\
                        .then_inc(o_free, 1)

                dve.sem_inc(s_free, 2)
                dve.sem_inc(o_free, 2)
                dve.memset(row_max[:, :, :], 0.0).then_inc(zeros_ready, 1)
                dve.wait_ge(zeros_ready, 1)
                for n in range(2):
                    for i in reversed(range(QT)):
                        reduce(n, n, i)
                    if n == 0:
                        negate(0, 0)
                with dve.Fori(0, N // R) as g:
                    for r in range(R):
                        n = g * R + r
                        for j in range(QT):
                            reduce(n + 2, (r + 2) % R, QT - 1 - j)
                            if j == 1:
                                negate(n + 1, (r + 1) % R)
                        if r > 0:
                            output(n - 1, r - 1)
                    output(n, R - 1)

        with nc.Block() as block:
            @block.sync
            def _(sp):
                for s in sems:
                    sp.sem_clear(s)


def out_phase(nc, name, o_sb, x_in, x_out, w_o, b_o, consts):
    ident = consts["ident"]
    biased = b_o is not None
    with ExitStack() as ctx:
        def sb(n, shape, dt=F32):
            return ctx.enter_context(nc.sbuf_tensor(f"{name}_{n}", shape, dt))

        def ps(n, shape, dt=F32):
            return ctx.enter_context(nc.psum_tensor(f"{name}_{n}", shape, dt))

        sems = []

        def sem(n):
            sems.append(ctx.enter_context(nc.semaphore(f"{name}_{n}")))
            return sems[-1]

        w_raw = sb("w_raw", [P, KD, D])
        w_hi = sb("w_hi", [P, KD, D], F32R)
        w_lo = sb("w_lo", [P, KD, D], F32R)
        b_row = sb("b_row", [P, D])
        x_sb = sb("x_sb", [P, 2, SUB, D])
        o_tok = sb("o_tok", [P, 2, SUB, D])
        oT_hi = sb("oT_hi", [P, 2, KD, TILE], F32R)
        oT_lo = sb("oT_lo", [P, 2, KD, TILE], F32R)
        t_ps = ps("t_ps", [P, 2, TILE])
        y_ps = ps("y_ps", [P, 2, 2, D])

        x_loaded = [sem("x_loaded0"), sem("x_loaded1")]
        x_stored = [sem("x_stored0"), sem("x_stored1")]
        w_loaded = sem("w_loaded")
        passed = sem("passed")
        w_hi_ready = sem("w_hi_ready")
        w_ready = sem("w_ready")
        tok_ready = sem("tok_ready")
        xb_ready = sem("xb_ready")
        t_full = sem("t_full")
        oh_ready = sem("oh_ready")
        t_free = sem("t_free")
        y_full = sem("y_full")
        y_free = sem("y_free")

        x_in_v = x_in.rearrange("(t s p) d -> t p s d", p=P, s=SUB)
        x_out_v = x_out.rearrange("(t s p) d -> t p s d", p=P, s=SUB)
        o_v = o_sb[:, :].rearrange("p (b h q d) -> p b h q d", b=BATCH, h=HEADS, q=QT)

        with nc.Block() as block:

            @block.sync
            def _(sp):
                def load(t, p):
                    sp.dma_start(x_sb[:, p, :, :], x_in_v[t, :, :, :]).then_inc(x_loaded[p], 16)

                sp.dma_start(w_raw[:, :, :], w_o.rearrange("(k p) o -> p k o", p=P)).then_inc(w_loaded, 16)
                if biased:
                    sp.dma_start(b_row[:, :], b_o.rearrange("(a d) -> a d", a=1).to_broadcast([P, D])).then_inc(w_loaded, 16)
                load(0, 0)
                load(1, 1)
                with sp.Fori(0, TILES // 2) as i:
                    for p in range(2):
                        t = 2 * i + p
                        sp.wait_ge(y_free, 2 * t + 4)
                        sp.dma_start(x_out_v[t, :, :, :], x_sb[:, p, :, :]).then_inc(x_stored[p], 16)
                        sp.wait_ge(x_stored[p], 16 * i + 16)
                        load((t + 2) % TILES, p)
                for p in range(2):
                    sp.wait_ge(x_loaded[p], 16 * (TILES // 2 + 1))

            @block.gpsimd
            def _(pool):
                with pool.Fori(0, TILES // 2) as i:
                    for q in range(2):
                        t = 2 * i + q
                        wait_alone(pool, t_free, 2 * t + 2, passed)
                        for s in range(SUB):
                            last = pool.tensor_copy(o_tok[:, q, s, :].rearrange("p (h d) -> p h d", h=HEADS),
                                                    o_v[:, i, :, q * SUB + s, :])
                        last.then_inc(tok_ready, 1)

            @block.tensor
            def _(pe):
                def split_mms(out, pairs):
                    for n, (a, b) in enumerate(pairs):
                        last = pe.matmul(out, a, b, start=(n == 0), stop=(n == len(pairs) - 1))
                    return last

                pe.wait_ge(w_ready, 1)
                with pe.Fori(0, TILES // 2) as i:
                    for q in range(2):
                        t = 2 * i + q
                        pe.wait_ge(tok_ready, t + 1)
                        for kd in range(KD):
                            pe.wait_ge(t_free, 2 * t + kd + 3)
                            for s in range(SUB):
                                last = pe.transpose(t_ps[:, kd, s * P:(s + 1) * P], o_tok[:, q, s, kd * P:(kd + 1) * P], ident[:, :])
                            last.then_inc(t_full, 1)
                        pe.wait_ge(t_free, 2 * t + 6)
                        for half in range(2):
                            pe.wait_ge(y_free, 2 * t + half + 1)
                            for s in range(2):
                                toks = slice((2 * half + s) * P, (2 * half + s + 1) * P)
                                pairs = []
                                for kd in range(KD):
                                    pairs += [(oT_hi[:, q, kd, toks], w_hi[:, kd, :]), (oT_hi[:, q, kd, toks], w_lo[:, kd, :]),
                                              (oT_lo[:, q, kd, toks], w_hi[:, kd, :])]
                                last = split_mms(y_ps[:, half, s, :], pairs)
                            last.then_inc(y_full, 1)

            @block.scalar
            def _(act):
                act.wait_ge(w_loaded, 32 if biased else 16)
                act.activation(w_hi[:, :, :], w_raw[:, :, :], ACT.Copy).then_inc(w_hi_ready, 1)
                with act.Fori(0, TILES // 2) as i:
                    for q in range(2):
                        t = 2 * i + q
                        for kd in range(KD):
                            act.wait_ge(t_full, 2 * t + kd + 1)
                            act.activation(oT_hi[:, q, kd, :], t_ps[:, kd, :], ACT.Copy).then_inc(oh_ready, 1)

            @block.vector
            def _(dve):
                dve.sem_inc(t_free, 4)
                dve.sem_inc(y_free, 2)
                dve.wait_ge(w_hi_ready, 1)
                dve.tensor_tensor(w_lo[:, :, :], w_raw[:, :, :], w_hi[:, :, :].bitcast(F32), ALU.subtract).then_inc(w_ready, 1)
                with dve.Fori(0, TILES // 2) as i:
                    for q in range(2):
                        t = 2 * i + q
                        if biased:
                            dve.wait_ge(x_loaded[q], 16 * i + 16)
                            for s in range(SUB):
                                last = dve.tensor_tensor(x_sb[:, q, s, :], x_sb[:, q, s, :], b_row[:, :], ALU.add)
                            last.then_inc(xb_ready, 1)
                        for kd in range(KD):
                            dve.wait_ge(oh_ready, 2 * t + kd + 1)
                            dve.tensor_tensor(oT_lo[:, q, kd, :], t_ps[:, kd, :], oT_hi[:, q, kd, :].bitcast(F32),
                                              ALU.subtract).then_inc(t_free, 1)
                        for half in range(2):
                            dve.wait_ge(y_full, 2 * t + half + 1)
                            if biased:
                                dve.wait_ge(xb_ready, t + 1)
                            else:
                                dve.wait_ge(x_loaded[q], 16 * i + 16)
                            xs = x_sb[:, q, 2 * half:2 * half + 2, :]
                            dve.tensor_tensor(xs, xs, y_ps[:, half, :, :], ALU.add).then_inc(y_free, 1)

        with nc.Block() as block:
            @block.sync
            def _(sp):
                for s in sems:
                    sp.sem_clear(s)


def make_constants(nc, ctx):
    def sb(n, shape, dt=F32):
        return ctx.enter_context(nc.sbuf_tensor(n, shape, dt))

    ident = sb("ident", [P, P])
    identb = sb("identb", [P, P], BF16)
    maskb = sb("maskb", [P, P], BF16)
    neg_half = sb("neg_half", [P, SUB])
    eps = sb("eps", [P, SUB])
    zeroed = ctx.enter_context(nc.semaphore("zeroed"))
    made = ctx.enter_context(nc.semaphore("made"))
    with nc.Block() as block:
        @block.gpsimd
        def _(pool):
            pool.memset(ident[:, :], 0.0).then_inc(zeroed, 1)
            pool.memset(identb[:, :], 0.0).then_inc(zeroed, 1)
            pool.memset(maskb[:, :], 0.0).then_inc(zeroed, 1)
            pool.memset(neg_half[:, :], -0.5).then_inc(zeroed, 1)
            pool.memset(eps[:, :], EPS).then_inc(zeroed, 1)
            pool.wait_ge(zeroed, 5)
            for m in (ident, identb):
                pool.affine_select(out=m[:, :], in_=m[:, :], compare_op=ALU.not_equal, fill=1.0, base=0,
                                   pattern=[[-1, P]], channel_multiplier=1).then_inc(made, 1)
            pool.affine_select(out=maskb[:, :], in_=maskb[:, :], compare_op=ALU.is_ge, fill=BIG, base=0,
                               pattern=[[-1, P]], channel_multiplier=1).then_inc(made, 1)
            pool.wait_ge(made, 3)
    return {"ident": ident, "identb": identb, "maskb": maskb, "eps": eps, "neg_half": neg_half}


def make_selectors(nc, name, sel):
    with ExitStack() as ctx:
        sel_raw = ctx.enter_context(nc.sbuf_tensor(f"{name}_sel_raw", [P, E * P], F32))
        made = ctx.enter_context(nc.semaphore(f"{name}_sel_made"))
        v = sel_raw[:, :].rearrange("p (e m) -> p e m", m=P)
        with nc.Block() as block:
            @block.gpsimd
            def _(pool):
                pool.memset(sel_raw[:, :], 0.0).then_inc(made, 1)
                pool.wait_ge(made, 1)
                for n in range(2):
                    pool.affine_select(out=v, in_=v, compare_op=ALU.not_equal, fill=1.0, base=-n * E,
                                       pattern=[[-1, E], [0, P]], channel_multiplier=1).then_inc(made, 1)
                    pool.wait_ge(made, n + 2)
                pool.tensor_copy(sel[:, :], sel_raw[:, :]).then_inc(made, 1)
                pool.wait_ge(made, 4)
        with nc.Block() as block:
            @block.sync
            def _(sp):
                sp.sem_clear(made)


def moe_phase(nc, name, x_in, x_out, w_router, we1, we3, we2, ws1, ws3, ws2, consts):
    HS = ws1.shape[1]

    def loads(c, raw):
        gate, up, down = (raw[:, k * D:(k + 1) * D] for k in range(3))
        cols = slice(c * P, (c + 1) * P)
        if c < HS // P:
            g_w, u_w, d_w = ws1[:, cols], ws3[:, cols], ws2[cols, :]
        else:
            e = c - HS // P
            g_w, u_w, d_w = we1[e, :, :], we3[e, :, :], we2[e, :, :]
        return [(gate.rearrange("p (k h) -> p k h", k=KD), g_w.rearrange("(k p) h -> p k h", p=P)),
                (up.rearrange("p (k h) -> p k h", k=KD), u_w.rearrange("(k p) h -> p k h", p=P)),
                (down, d_w)]

    with nc.sbuf_tensor(f"{name}_sel", [P, E * P], F32R) as sel:
        make_selectors(nc, name, sel)
        ffn_phase(nc, name, x_in, x_out, HS // P + E, loads,
                  {"shared": 0.5 / (TOP_K + 1), "routed": 0.5 * TOP_K / (TOP_K + 1)}, {**consts, "sel": sel}, w_router)


def lookup_phase(nc, name, lut, idx, w_dram, chunks):
    INTER = idx[0].shape[1]
    LUT = lut.shape[0]
    PAD = chunks * P
    W = PAD * KD
    full = INTER // P
    rest = INTER - full * P
    with ExitStack() as ctx:
        def sb(n, shape, dt=F32):
            return ctx.enter_context(nc.sbuf_tensor(f"{name}_{n}", shape, dt))

        sems = []

        def sem(n):
            sems.append(ctx.enter_context(nc.semaphore(f"{name}_{n}")))
            return sems[-1]

        lut_row = sb("lut_row", [P, LUT])
        idx_sb = sb("idx_sb", [P, 3, W], I32)
        idx_f = sb("idx_f", [P, 3, W])
        term = sb("term", [P, 3, 2, W])
        w = sb("w", [P, 3, W])
        idx_zeroed = sem("idx_zeroed")
        loaded = sem("loaded")
        idx_ready = sem("idx_ready")
        term_ready = [sem(f"term_ready{m}") for m in range(3)]
        sum_ready = [sem(f"sum_ready{m}") for m in range(3)]
        stored = sem("stored")
        with nc.Block() as block:

            @block.sync
            def _(sp):
                n = 0
                sp.wait_ge(idx_zeroed, 3)
                sp.dma_start(lut_row[:, :], lut.rearrange("(a n) -> a n", a=1).to_broadcast([P, LUT])).then_inc(loaded, 16)
                for m in range(2):
                    v = idx_sb[:, m, :].rearrange("p (k h) -> p k h", k=KD)
                    sp.dma_start(v[:, :, 0:INTER], idx[m].rearrange("(k p) h -> p k h", p=P)).then_inc(loaded, 16)
                v = idx_sb[:, 2, :].rearrange("p (c d) -> p c d", c=chunks)
                sp.dma_start(v[:, 0:full, :], idx[2][0:full * P, :].rearrange("(c p) d -> p c d", p=P)).then_inc(loaded, 16)
                if rest:
                    sp.dma_start(v[0:rest, full, :], idx[2][full * P:INTER, :]).then_inc(loaded, 16)
                for m in range(3):
                    sp.wait_ge(sum_ready[m], LUT)
                    if m < 2:
                        src = w[:, m, :].rearrange("p (k c h) -> p c k h", k=KD, c=chunks)
                        for c in range(chunks):
                            dst = w_dram[c, :, m * D:(m + 1) * D].rearrange("p (k h) -> p k h", k=KD)
                            sp.dma_start(dst, src[:, c, :, :]).then_inc(stored, 16)
                            n += 1
                    else:
                        src = w[:, m, :].rearrange("p (c d) -> p c d", c=chunks)
                        for c in range(chunks):
                            sp.dma_start(w_dram[c, :, m * D:(m + 1) * D], src[:, c, :]).then_inc(stored, 16)
                            n += 1
                sp.wait_ge(stored, 16 * n)

            @block.gpsimd
            def _(pool):
                for m in range(3):
                    pool.memset(idx_sb[:, m, :], -1).then_inc(idx_zeroed, 1)

            @block.vector
            def _(dve):
                dve.wait_ge(loaded, 16 * (5 if rest else 4))
                for m in range(3):
                    dve.tensor_copy(idx_f[:, m, :], idx_sb[:, m, :]).then_inc(idx_ready, 1)
                dve.wait_ge(idx_ready, 3)
                for k in range(LUT):
                    for m in range(3):
                        if k >= 2:
                            dve.wait_ge(sum_ready[m], k - 1)
                        out = w[:, m, :] if k == 0 else term[:, m, k % 2, :]
                        dve.tensor_scalar(out, idx_f[:, m, :], float(k), lut_row[:, k:k + 1], ALU.is_equal, ALU.mult)\
                            .then_inc(sum_ready[m] if k == 0 else term_ready[m], 1)
                    if k:
                        for m in range(3):
                            dve.wait_ge(term_ready[m], k)
                            dve.wait_ge(sum_ready[m], k)
                            dve.tensor_tensor(w[:, m, :], w[:, m, :], term[:, m, k % 2, :], ALU.add).then_inc(sum_ready[m], 1)

        with nc.Block() as block:
            @block.sync
            def _(sp):
                for s in sems:
                    sp.sem_clear(s)


def lut_phase(nc, name, x_in, x_out, w_dram, chunks, consts):
    def loads(c, raw):
        return [(raw, w_dram[c, :, :])]

    with nc.sbuf_tensor(f"{name}_sel", [P, 2], F32R) as sel:
        ffn_phase(nc, name, x_in, x_out, chunks, loads, {"shared": 0.5}, {**consts, "sel": sel})


def attention_phase(nc, name, x_in, x_out, q_dram, k_dram, w_qkv, b_qkv, w_o, b_o, consts):
    by_head = "b h l d t -> (b h) l d t"
    with nc.sbuf_tensor(f"{name}_o_sb", [P, BATCH * HEADS * QT * HD], F32) as o_sb:
        with nc.sbuf_tensor(f"{name}_v_sb", [P, BATCH * HEADS * QT * VW], F32) as v_sb:
            project_phase(nc, f"{name}_proj", x_in, w_qkv, b_qkv, q_dram, k_dram, v_sb, consts)
            heads_phase(nc, f"{name}_heads", q_dram.rearrange(by_head), k_dram.rearrange(by_head), v_sb, o_sb, consts)
        out_phase(nc, f"{name}_out", o_sb, x_in, x_out, w_o, b_o, consts)


def macaron(nc, t, out):
    def dram(name, shape, dt=F32):
        return nc.dram_tensor(name, shape, dt, kind="Internal").ap()

    INTER = t["L1_ffn_gate_idx"].shape[1]
    CHUNKS = -(-INTER // P)
    x1, x2, x3, x4, x5 = (dram(f"x{n}", [TOK, D]) for n in range(1, 6))
    q_dram = dram("q_dram", [BATCH, HEADS, 2, HD, SEQ])
    k_dram = dram("k_dram", [BATCH, HEADS, 2, HD, SEQ])
    w_dram = dram("w_dram", [CHUNKS, P, 3 * D])
    moe = [t[f"L0_ffn_{w}"] for w in ("w_router", "we1", "we3", "we2", "ws1", "ws3", "ws2")]
    with ExitStack() as ctx:
        consts = make_constants(nc, ctx)
        moe_phase(nc, "moe0", t["L0_attn_x"], x1, *moe, consts)
        attention_phase(nc, "attn0", x1, x2, q_dram, k_dram, [t[f"L0_attn_W{w}"] for w in "qkv"],
                        [t[f"L0_attn_b{w}"] for w in "qkv"], t["L0_attn_Wo"], t["L0_attn_bo"], consts)
        moe_phase(nc, "moe1", x2, x3, *moe, consts)
        lookup_phase(nc, "lookup", t["L1_ffn_lut"], [t[f"L1_ffn_{w}_idx"] for w in ("gate", "up", "down")], w_dram, CHUNKS)
        lut_phase(nc, "lut0", x3, x4, w_dram, CHUNKS, consts)
        attention_phase(nc, "attn1", x4, x5, q_dram, k_dram, [t[f"L1_attn_W{w}"] for w in "qkv"], None,
                        t["L1_attn_Wp"], None, consts)
        lut_phase(nc, "lut1", x5, out, w_dram, CHUNKS, consts)


_INS = ['L0_attn_x', 'L0_attn_Wq T', 'L0_attn_bq', 'L0_attn_Wk T', 'L0_attn_bk', 'L0_attn_Wv T', 'L0_attn_bv', 'L0_attn_Wo T',
        'L0_attn_bo', 'L0_ffn_w_router', 'L0_ffn_we1', 'L0_ffn_we3', 'L0_ffn_we2', 'L0_ffn_ws1', 'L0_ffn_ws3', 'L0_ffn_ws2',
        'L1_attn_Wq T', 'L1_attn_Wk T', 'L1_attn_Wv T', 'L1_attn_Wp T', 'L1_ffn_lut', 'L1_ffn_gate_idx T', 'L1_ffn_up_idx T',
        'L1_ffn_down_idx T']


def kernel(**inputs):
    import numpy as _np
    import concourse.bacc as _bacc
    from concourse import mybir as _mybir
    from concourse.bass_utils import run_bass_kernel_spmd as _run

    nc = _bacc.Bacc("TRN2", target_bir_lowering=False, num_devices=1)
    arrays, tensors = {}, {}
    shape = inputs['L0_attn_x'].shape
    for entry in _INS:
        name, _, turned = entry.partition(" ")
        a = _np.asarray(inputs[name])
        if turned:
            a = a.T
        if name == 'L0_attn_x':
            a = a.reshape(-1, a.shape[-1])
        a = _np.ascontiguousarray(a)
        arrays[f"in_{name}_dram"] = a
        tensors[name] = nc.dram_tensor(f"in_{name}_dram", a.shape, _mybir.dt.from_np(a.dtype), kind="ExternalInput").ap()
    out = nc.dram_tensor("out_0_dram", (TOK, D), _mybir.dt.from_np(_np.dtype("float32")), kind="ExternalOutput").ap()
    macaron(nc, tensors, out)
    r = _run(nc, [arrays], core_ids=[0])
    return r.results[0]["out_0_dram"].reshape(shape)
```

```python
import concourse.bass as bass
from concourse import mybir
from contextlib import ExitStack

ALU = mybir.AluOpType
ACT = mybir.ActivationFunctionType
AX = mybir.AxisListType
F32 = mybir.dt.float32
F32R = mybir.dt.float32r
BF16 = mybir.dt.bfloat16
I32 = mybir.dt.int32

P = 128
TOK = 4096
D = 256
KD = D // P
TILE = 512
SUB = TILE // P
TILES = TOK // TILE
E = 16
TOP_K = 4
EPS = 1e-5


def wait_alone(engine, sem, value, passed):
    engine.wait_ge(sem, value)
    engine.sem_inc(passed, 1)


def layer_norm_moments(dve, x, stats, moments, stats_done, moments_done, passed, n):
    for s in range(SUB):
        last = dve.bn_stats(stats[:, s, :], x[:, s, :])
    last.then_inc(stats_done, 1)
    wait_alone(dve, stats_done, n + 1, passed)
    for s in range(SUB):
        last = dve.bn_aggr(moments[:, s, :], stats[:, s, :])
    last.then_inc(moments_done, 1)


def is_first(n):
    return isinstance(n, int) and n == 0


def ffn_phase(nc, name, x_in, x_out, chunks, weight_loads, gain, consts, w_router=None, lookup=None):
    routed = w_router is not None
    shared = chunks - (E if routed else 0)
    NC = chunks
    FRONT = 4 if routed else 2
    USES = FRONT + 2
    if routed:
        AT = {"stats": 1, "norm": 3, "x0": 5, "x1": 6, "logits": 8, "route": 9, "top": 10, "cw": 14}
    else:
        AT = {"stats": 0, "norm": 1, "x0": 3, "x1": 4, "logits": -1, "route": -1, "top": -1, "cw": -1}
    HB = 4 if NC % 4 == 0 else 3
    assert NC % HB == 0 and NC % 2 == 0
    EARLY = NC * 2 // 5
    ident, eps, neg_half = consts["ident"], consts["eps"], consts["neg_half"]

    with ExitStack() as ctx:
        def sb(n, shape, dt=F32):
            return ctx.enter_context(nc.sbuf_tensor(f"{name}_{n}", shape, dt))

        def ps(n, shape, dt=F32):
            return ctx.enter_context(nc.psum_tensor(f"{name}_{n}", shape, dt))

        def sem(n):
            return ctx.enter_context(nc.semaphore(f"{name}_{n}"))

        w_hi = sb("w_hi", [P, NC, 3 * D], F32R)
        w_lo = sb("w_lo", [P, NC, 3 * D], F32R)
        RAW = 4
        w_raw = sb("w_raw", [P, RAW, 3 * D])
        x_sb = sb("x_sb", [P, SUB, D])
        sum_sb = sb("sum_sb", [P, SUB, D])
        xn = sb("xn", [P, SUB, D])
        stats = sb("stats", [P, SUB, 6])
        moments = sb("moments", [P, SUB, 2])
        var_eps = sb("var_eps", [P, SUB])
        rstd = sb("rstd", [P, SUB])
        xT_hi = sb("xT_hi", [P, 2, KD, TILE], F32R)
        xT_lo = sb("xT_lo", [P, 2, KD, TILE], F32R)
        gate = sb("gate", [P, 2, TILE])
        hid0 = sb("hid0", [P, TILE])
        hid = sb("hid", [P, 2, TILE])
        h_hi = sb("h_hi", [P, HB, TILE], F32R)
        h_lo = sb("h_lo", [P, HB, TILE], F32R)
        yT = sb("yT", [P, KD, TILE])
        if routed:
            wr_raw = sb("wr_raw", [P, KD, E])
            wr = sb("wr", [P, 2, KD, E], F32R)
            top_in = sb("top_in", [P, SUB, E + TOP_K])
            top_out = sb("top_out", [P, SUB, E + TOP_K])
            shifted = sb("shifted", [P, SUB, E])
            row_max = sb("row_max", [P, SUB])
            top8 = sb("top8", [P, SUB, 8])
            top_sum = sb("top_sum", [P, SUB])
            inv_sum = sb("inv_sum", [P, SUB])
            cw_raw = sb("cw_raw", [P, SUB, E])
            cw = sb("cw", [P, SUB, E])
            cw_parts = sb("cw_parts", [P, SUB, P])
            cwT = sb("cwT", [P, 2, TILE], F32R)
            sel = sb("sel", [P, E * P], F32R)
        g_ps = ps("g_ps", [P, 2, TILE])
        u_ps = ps("u_ps", [P, 2, TILE])
        y_ps = ps("y_ps", [P, KD, TILE])
        c_ps = ps("c_ps", [P, TILE])
        t_ps = ps("t_ps", [P, TILE])

        x_loaded = sem("x_loaded")
        sum_loaded = sem("sum_loaded")
        x_stored = sem("x_stored")
        raw_loaded = [sem(f"raw_loaded{r}") for r in range(RAW)]
        w_hi_ready = sem("w_hi_ready")
        w_ready = sem("w_ready")
        early_hi_ready = sem("early_hi_ready")
        early_ready = sem("early_ready")
        stats_done = sem("stats_done")
        moments_done = sem("moments_done")
        var_done = sem("var_done")
        rstd_ready = sem("rstd_ready")
        xn_ready = sem("xn_ready")
        xh_ready = sem("xh_ready")
        passed = sem("passed")
        t_full = sem("t_full")
        t_free = sem("t_free")
        g_full = sem("g_full")
        u_full = sem("u_full")
        c_full = sem("c_full")
        gate_ready = sem("gate_ready")
        hid0_ready = sem("hid0_ready")
        hid_ready = sem("hid_ready")
        hh_ready = sem("hh_ready")
        h_ready = sem("h_ready")
        h_used = sem("h_used")
        y0_free = sem("y0_free")
        y1_free = sem("y1_free")
        sems = [x_stored, x_loaded, sum_loaded, *raw_loaded, w_hi_ready, w_ready, early_hi_ready, early_ready, stats_done, moments_done, var_done, rstd_ready,
                xn_ready, xh_ready, passed, t_full, t_free, g_full, u_full, c_full, gate_ready, hid0_ready,
                hid_ready, hh_ready, h_ready, h_used, y0_free, y1_free]
        if routed:
            wr_loaded = sem("wr_loaded")
            wr_hi_ready = sem("wr_hi_ready")
            wr_ready = sem("wr_ready")
            pads_ready = sem("pads_ready")
            max_ready = sem("max_ready")
            exp_ready = sem("exp_ready")
            route_step = sem("route_step")
            cw_ready = sem("cw_ready")
            sel_made = sem("sel_made")
            sems += [sel_made, wr_loaded, wr_hi_ready, wr_ready, pads_ready, max_ready, exp_ready, route_step, cw_ready]

        if lookup:
            lut, idx, w_dram, lookup_chunks, (lut_loaded, idx_loaded, lookup_stored) = lookup
            LUT = lut.shape[0]
            INTER = idx[0].shape[1]
            lut_row = sb("lut_row", [P, LUT])
            idx_int, idx_f, term, found = w_raw[:, 0, :].bitcast(I32), w_raw[:, 1, :], w_raw[:, 2, :], w_raw[:, 3, :]
            idx_padded = sem("idx_padded")
            idx_ready = sem("idx_ready")
            term_ready = sem("term_ready")
            sum_ready = sem("sum_ready")
            pool_passed = sem("pool_passed")
            sems += [idx_padded, idx_ready, term_ready, sum_ready, pool_passed]

        x_in_v = x_in.rearrange("(t s p) d -> t p s d", p=P, s=SUB)
        x_out_v = x_out.rearrange("(t s p) d -> t p s d", p=P, s=SUB)

        def wait_split(engine, c):
            if c < EARLY:
                engine.wait_ge(early_ready, c + 1)
            else:
                engine.wait_ge(w_ready, c - EARLY + 1)

        def wait_raw(engine, c):
            before = range(c % RAW, c + 1, RAW)
            engine.wait_ge(raw_loaded[c % RAW], 16 * sum(len(weight_loads(b, w_raw[:, 0, :])) for b in before))

        with nc.Block() as block:

            @block.sync
            def _(sp):
                sp.dma_start(x_sb[:, :, :], x_in_v[0, :, :, :]).then_inc(x_loaded, 16)
                if routed:
                    sp.dma_start(wr_raw[:, :, :], w_router.rearrange("(k p) e -> p k e", p=P)).then_inc(wr_loaded, 16)
                sp.dma_start(sum_sb[:, :, :], x_in_v[0, :, :, :]).then_inc(sum_loaded, 16)
                for c in range(NC):
                    if c >= RAW:
                        wait_split(sp, c - RAW)
                    for dst, src in weight_loads(c, w_raw[:, c % RAW, :]):
                        sp.dma_start(dst, src).then_inc(raw_loaded[c % RAW], 16)
                    if c == RAW - 1:
                        sp.wait_ge(xn_ready, 1)
                        sp.dma_start(x_sb[:, :, :], x_in_v[1, :, :, :]).then_inc(x_loaded, 16)
                with sp.Fori(0, TILES) as t:
                    sp.wait_ge(xn_ready, t + 2)
                    sp.dma_start(x_sb[:, :, :], x_in_v[(t + 2) % TILES, :, :, :]).then_inc(x_loaded, 16)
                    sp.wait_ge(t_free, (t + 1) * USES + FRONT)
                    sp.dma_start(x_out_v[t, :, :, :], sum_sb[:, :, :]).then_inc(x_stored, 16)
                    sp.wait_ge(x_stored, 16 * t + 16)
                    sp.dma_start(sum_sb[:, :, :], x_in_v[(t + 1) % TILES, :, :, :]).then_inc(sum_loaded, 16)
                sp.wait_ge(x_loaded, 16 * (TILES + 2))
                sp.wait_ge(sum_loaded, 16 * (TILES + 1))

            @block.gpsimd
            def _(pool):
                def rstd_of(n):
                    pool.wait_ge(moments_done, n + 1)
                    pool.tensor_tensor(var_eps[:, :], moments[:, :, 1], eps[:, :], ALU.add).then_inc(var_done, 1)
                    pool.wait_ge(var_done, n + 1)
                    pool.tensor_tensor(rstd[:, :], var_eps[:, :], neg_half[:, :], ALU.pow).then_inc(rstd_ready, 1)

                rstd_of(0)
                if routed:
                    pool.wait_ge(wr_loaded, 16)
                    pool.tensor_copy(wr[:, 0, :, :], wr_raw[:, :, :]).then_inc(wr_hi_ready, 1)
                    pool.wait_ge(wr_hi_ready, 1)
                    pool.tensor_tensor(wr[:, 1, :, :], wr_raw[:, :, :], wr[:, 0, :, :].bitcast(F32),
                                       ALU.subtract).then_inc(wr_ready, 1)
                    HE = E // 2
                    for half in range(2):
                        made = half * 4
                        v = yT[:, :, :].rearrange("p a (e m) -> p (a e) m", m=P)
                        pool.memset(v, 0.0).then_inc(sel_made, 1)
                        for n in range(2):
                            pool.wait_ge(sel_made, made + n + 1)
                            pool.affine_select(out=v, in_=v, compare_op=ALU.not_equal, fill=1.0, base=-(n * E + half * HE),
                                               pattern=[[-1, HE], [0, P]], channel_multiplier=1).then_inc(sel_made, 1)
                        pool.wait_ge(sel_made, made + 3)
                        pool.tensor_copy(sel[:, half * HE * P:(half + 1) * HE * P].rearrange("p (e m) -> p e m", m=P), v)\
                            .then_inc(sel_made, 1)
                        pool.wait_ge(sel_made, made + 4)
                for c in range(EARLY, NC):
                    wait_raw(pool, c)
                    pool.tensor_copy(w_hi[:, c, :], w_raw[:, c % RAW, :]).then_inc(w_hi_ready, 1)
                    pool.wait_ge(w_hi_ready, c - EARLY + 1)
                    pool.tensor_tensor(w_lo[:, c, :], w_raw[:, c % RAW, :], w_hi[:, c, :].bitcast(F32),
                                       ALU.subtract).then_inc(w_ready, 1)
                    if c == EARLY:
                        rstd_of(1)

                def look_up(b, rows):
                    rstd_of(2 * b + 2)
                    c = lookup_chunks[0] + b
                    gate_up = idx_int[:, 0:2 * D].rearrange("p (m k h) -> p m k h", m=2, k=KD)
                    for m in range(2):
                        pool.dma_start(gate_up[:, m, :, 0:rows],
                                       idx[m].rearrange("(k p) h -> p k h", p=P)[:, :, bass.ds(c * P, rows)])\
                            .then_inc(idx_loaded, 16)
                    pool.dma_start(idx_int[0:rows, 2 * D:3 * D], idx[2][bass.ds(c * P, rows), :]).then_inc(idx_loaded, 16)
                    wait_alone(pool, idx_loaded, 48 * b + 48, pool_passed)
                    pool.tensor_copy(idx_f, idx_int).then_inc(idx_ready, 1)
                    wait_alone(pool, idx_ready, b + 1, pool_passed)
                    for k in range(LUT):
                        if k == LUT // 2:
                            rstd_of(2 * b + 3)
                        if k > 1:
                            wait_alone(pool, sum_ready, b * LUT + k, pool_passed)
                        pool.tensor_scalar(term if k else found, idx_f, float(k), lut_row[:, k:k + 1], ALU.is_equal, ALU.mult)\
                            .then_inc(term_ready if k else sum_ready, 1)
                        if k:
                            pool.wait_ge(term_ready, b * (LUT - 1) + k)
                            pool.wait_ge(sum_ready, b * LUT + k)
                            pool.tensor_tensor(found, found, term, ALU.add).then_inc(sum_ready, 1)
                    pool.wait_ge(sum_ready, b * LUT + LUT)
                    pool.dma_start(w_dram[c, :, :], found).then_inc(lookup_stored, 16)
                    pool.wait_ge(lookup_stored, 16 * b + 16)

                done = 0
                if lookup:
                    pool.dma_start(lut_row[:, :], lut.rearrange("(a n) -> a n", a=1).to_broadcast([P, LUT]))\
                        .then_inc(lut_loaded, 16)
                    pool.wait_ge(w_ready, NC - EARLY)
                    pool.wait_ge(lut_loaded, 16)
                    full = sum((c + 1) * P <= INTER for c in lookup_chunks)
                    with pool.Fori(0, full) as b:
                        look_up(b, P)
                    if full < len(lookup_chunks):
                        pool.memset(idx_int, -1).then_inc(idx_padded, 1)
                        pool.wait_ge(idx_padded, 1)
                        look_up(full, INTER - lookup_chunks[-1] * P)
                    done = 2 * len(lookup_chunks)
                with pool.Fori(2 + done, TILES + 1) as n:
                    rstd_of(n)

            def front_steps(step):
                return [k for k, at in AT.items() if at == step]

            @block.tensor
            def _(pe):
                def split_mms(out, pairs, start, stop):
                    for n, (a, b) in enumerate(pairs):
                        last = pe.matmul(out, a, b, start=(start and n == 0), stop=(stop and n == len(pairs) - 1))
                    return last

                def use_bank(use):
                    pe.wait_ge(t_free, use)

                def x_turn(n, use, kd):
                    pe.wait_ge(xn_ready, n + 1)
                    for s in range(SUB):
                        last = pe.transpose(t_ps[:, s * P:(s + 1) * P], xn[:, s, kd * P:(kd + 1) * P], ident[:, :])
                    last.then_inc(t_full, 1)

                def logits(q, use):
                    for s in range(SUB):
                        pairs = []
                        for kd in range(KD):
                            for a, b in ((xT_hi, 0), (xT_hi, 1), (xT_lo, 0), (xT_lo, 1)):
                                pairs.append((a[:, q, kd, s * P:(s + 1) * P], wr[:, b, kd, :]))
                        last = split_mms(t_ps[:, s * E:(s + 1) * E], pairs, True, True)
                    last.then_inc(t_full, 1)

                def cw_turn(n):
                    pe.wait_ge(cw_ready, n + 1)
                    for s in range(SUB):
                        last = pe.transpose(t_ps[:, s * P:(s + 1) * P], cw_parts[:, s, :], ident[:, :])
                    last.then_inc(t_full, 1)

                def front(n, q, use, steps):
                    for k in steps:
                        if k == "x0":
                            if not isinstance(use, int) or use > 0:
                                use_bank(use)
                            x_turn(n, use, 0)
                        if k == "x1":
                            use_bank(use + 1)
                            x_turn(n, use + 1, 1)
                        if k == "logits" and routed:
                            use_bank(use + 2)
                            logits(q, use + 2)
                        if k == "cw" and routed:
                            use_bank(use + 3)
                            cw_turn(n)

                def gate_up(g, q, c):
                    b = c % 2
                    wait_split(pe, c)
                    pe.wait_ge(hid_ready, g + 1)
                    for ps_, off, full in ((g_ps, 0, g_full), (u_ps, D, u_full)):
                        pairs = []
                        for kd in range(KD):
                            cols = slice(off + kd * P, off + (kd + 1) * P)
                            pairs += [(w_hi[:, c, cols], xT_hi[:, q, kd, :]), (w_hi[:, c, cols], xT_lo[:, q, kd, :]),
                                      (w_lo[:, c, cols], xT_hi[:, q, kd, :])]
                        split_mms(ps_[:, b, :], pairs, True, True).then_inc(full, 1)

                def spread_weight(g, q, c):
                    pe.wait_ge(hid_ready, g + 2)
                    pe.matmul(c_ps[:, :], sel[:, (c - shared) * P:(c - shared + 1) * P], cwT[:, q, :],
                              start=True, stop=True).then_inc(c_full, 1)

                def down(g, c):
                    b = c % HB
                    pe.wait_ge(h_ready, g + 3)
                    for m in range(KD):
                        cols = slice(2 * D + m * P, 2 * D + (m + 1) * P)
                        last = split_mms(y_ps[:, m, :], [(w_hi[:, c, cols], h_hi[:, b, :]), (w_hi[:, c, cols], h_lo[:, b, :]),
                                                         (w_lo[:, c, cols], h_hi[:, b, :])], c == 0, c == NC - 1)
                    last.then_inc(h_used, 1)

                pe.sem_inc(h_used, HB)
                if routed:
                    pe.wait_ge(wr_ready, 1)
                front(0, 0, 0, list(AT))

                def y_turn(use, half):
                    use_bank(use + half)
                    for s in range(2):
                        for m in range(KD):
                            last = pe.transpose(t_ps[:, s * D + m * P:s * D + (m + 1) * P],
                                                yT[:, m, (2 * half + s) * P:(2 * half + s + 1) * P], ident[:, :])
                    last.then_inc(t_full, 1)

                def y_copied(t):
                    pe.wait_ge(y0_free, t + 1)
                    pe.wait_ge(y1_free, t + 1)

                def tile(i, q):
                    t = 2 * i + q
                    use = t * USES + FRONT
                    pe.wait_ge(t_free, use if is_first(t) else use - 2)
                    for c in range(NC):
                        g = t * NC + c
                        gate_up(g, q, c)
                        if c >= shared:
                            if c == shared and is_first(t):
                                pe.wait_ge(sel_made, 8)
                            spread_weight(g, q, c)
                        if c < 2 and not is_first(t):
                            down(g - 2, NC - 2 + c)
                        if c == 2:
                            y_copied(t)
                            if not is_first(t):
                                y_turn(use - 2, 0)
                        if c >= 2:
                            down(g - 2, c - 2)
                        if c == 2 and not is_first(t):
                            y_turn(use - 2, 1)
                        front(t + 1, 1 - q, use, front_steps(c))

                for q in range(2):
                    tile(0, q)
                with pe.Fori(1, TILES // 2) as i:
                    for q in range(2):
                        tile(i, q)
                for c in (NC - 2, NC - 1):
                    down((TILES - 1) * NC + c, c)
                y_copied(TILES)
                for half in range(2):
                    y_turn(TILES * USES + FRONT - 2, half)

            @block.scalar
            def _(act):
                def front(n, q, use, steps):
                    for k in steps:
                        if k in ("x0", "x1"):
                            kd = int(k[1])
                            act.wait_ge(t_full, use + kd + 1)
                            act.activation(xT_hi[:, q, kd, :], t_ps[:, :], ACT.Copy).then_inc(xh_ready, 1)
                        if k == "route" and routed:
                            act.wait_ge(t_free, use + 3)
                            act.activation(top_in[:, :, 0:E], shifted[:, :, :], ACT.Exp).then_inc(exp_ready, 1)
                        if k == "cw" and routed:
                            act.wait_ge(t_full, use + 4)
                            act.activation(cwT[:, q, :], t_ps[:, :], ACT.Copy).then_inc(t_free, 1)

                def hidden_hi(g, c):
                    act.wait_ge(hid_ready, g + 3)
                    act.wait_ge(h_used, g + 1)
                    act.activation(h_hi[:, c % HB, :], hid[:, c % 2, :], ACT.Copy).then_inc(hh_ready, 1)

                act.sem_inc(y0_free, 1)
                for c in range(EARLY):
                    wait_raw(act, c)
                    act.activation(w_hi[:, c, :], w_raw[:, c % RAW, :], ACT.Copy).then_inc(early_hi_ready, 1)
                    if c == 0:
                        front(0, 0, 0, list(AT))

                def copy_y(t):
                    act.wait_ge(h_used, HB + t * NC)
                    act.activation(yT[:, 0, :], y_ps[:, 0, :], ACT.Copy).then_inc(y0_free, 1)

                def tile(i, q):
                    t = 2 * i + q
                    for c in range(NC):
                        g = t * NC + c
                        act.wait_ge(g_full, g + 1)
                        act.activation(gate[:, c % 2, :], g_ps[:, c % 2, :], ACT.Silu).then_inc(gate_ready, 1)
                        if c >= 1 or not is_first(t):
                            hidden_hi(g - 1, (c - 1) % NC)
                        if c == 1 and not is_first(t):
                            copy_y(t)
                        front(t + 1, 1 - q, t * USES + FRONT, front_steps(c))

                for q in range(2):
                    tile(0, q)
                with act.Fori(1, TILES // 2) as i:
                    for q in range(2):
                        tile(i, q)
                hidden_hi(TILES * NC - 1, NC - 1)
                copy_y(TILES)

            @block.vector
            def _(dve):
                def front(n, q, use, steps):
                    for k in steps:
                        if k == "stats":
                            dve.wait_ge(x_loaded, 16 * n + 16)
                            layer_norm_moments(dve, x_sb[:, :, :], stats, moments, stats_done, moments_done, passed, n)
                        if k == "norm":
                            dve.wait_ge(rstd_ready, n + 1)
                            for s in range(SUB):
                                last = dve.tensor_scalar(xn[:, s, :], x_sb[:, s, :], moments[:, s, 0:1], rstd[:, s:s + 1],
                                                         ALU.subtract, ALU.mult)
                            last.then_inc(xn_ready, 1)
                        if k in ("x0", "x1"):
                            kd = int(k[1])
                            dve.wait_ge(xh_ready, 2 * n + kd + 1)
                            dve.tensor_tensor(xT_lo[:, q, kd, :], t_ps[:, :], xT_hi[:, q, kd, :].bitcast(F32),
                                              ALU.subtract).then_inc(t_free, 1)
                        if k == "route" and routed:
                            logit = t_ps[:, 0:SUB * E].rearrange("p (s e) -> p s e", e=E)
                            dve.wait_ge(t_full, use + 3)
                            dve.tensor_reduce(row_max[:, :], logit, AX.X, ALU.max).then_inc(max_ready, 1)
                            dve.wait_ge(max_ready, n + 1)
                            dve.tensor_tensor(shifted[:, :, :], logit, row_max[:, :].unsqueeze(2).to_broadcast([P, SUB, E]),
                                              ALU.subtract).then_inc(t_free, 1)
                        if k == "top" and routed:
                            wait_alone(dve, exp_ready, n + 1, passed)
                            for s in range(SUB):
                                last = dve.max(top8[:, s, :], top_in[:, s, :])
                            last.then_inc(route_step, 1)
                            dve.wait_ge(route_step, n * 7 + 1)
                            dve.tensor_reduce(top_sum[:, :], top8[:, :, 0:TOP_K], AX.X, ALU.add).then_inc(route_step, 1)
                            dve.memset(top8[:, :, TOP_K:8], -1.0).then_inc(route_step, 1)
                            dve.wait_ge(route_step, n * 7 + 3)
                            dve.reciprocal(inv_sum[:, :], top_sum[:, :])
                            for s in range(SUB):
                                last = dve.match_replace(top_out[:, s, :], top8[:, s, :], top_in[:, s, :], 0.0)
                            last.then_inc(route_step, 1)
                            dve.wait_ge(route_step, n * 7 + 4)
                            dve.tensor_tensor(cw_raw[:, :, :], top_in[:, :, 0:E], top_out[:, :, 0:E], ALU.subtract)\
                               .then_inc(route_step, 1)
                            dve.wait_ge(route_step, n * 7 + 5)
                            for s in range(SUB):
                                last = dve.tensor_scalar(cw[:, s, :], cw_raw[:, s, :], inv_sum[:, s:s + 1], gain["routed"],
                                                         ALU.mult, ALU.mult)
                            last.then_inc(route_step, 1)
                            dve.wait_ge(route_step, n * 7 + 6)
                            dve.tensor_copy(cw_parts[:, :, 0:E].bitcast(F32R), cw[:, :, :]).then_inc(route_step, 1)
                            dve.wait_ge(route_step, n * 7 + 7)
                            dve.tensor_tensor(cw_parts[:, :, E:2 * E], cw[:, :, :], cw_parts[:, :, 0:E], ALU.subtract)\
                               .then_inc(cw_ready, 1)

                def product(g, c, t):
                    b = c % 2
                    dve.wait_ge(gate_ready, g + 1)
                    dve.wait_ge(u_full, g + 1)
                    dve.wait_ge(h_ready, g + 1)
                    if c < shared:
                        dve.scalar_tensor_tensor(out=hid[:, b, :], in0=gate[:, b, :], scalar=gain["shared"], in1=u_ps[:, b, :],
                                                 op0=ALU.mult, op1=ALU.mult).then_inc(hid_ready, 1)
                    else:
                        n = t * E + (c - shared) + 1
                        dve.wait_ge(hid_ready, g + 2)
                        dve.tensor_tensor(hid0[:, :], gate[:, b, :], u_ps[:, b, :], ALU.mult).then_inc(hid0_ready, 1)
                        dve.wait_ge(hid0_ready, n)
                        dve.wait_ge(c_full, n)
                        dve.tensor_tensor(hid[:, b, :], hid0[:, :], c_ps[:, :], ALU.mult).then_inc(hid_ready, 1)

                def hidden_lo(g, c):
                    dve.wait_ge(hh_ready, g + 1)
                    dve.tensor_tensor(h_lo[:, c % HB, :], hid[:, c % 2, :], h_hi[:, c % HB, :].bitcast(F32),
                                      ALU.subtract).then_inc(h_ready, 1)

                dve.sem_inc(hid_ready, 2)
                dve.sem_inc(h_ready, 2)
                dve.sem_inc(y1_free, 1)
                if routed:
                    dve.memset(cw_parts[:, :, :], 0.0).then_inc(pads_ready, 1)
                    dve.memset(top_in[:, :, E:], -1.0).then_inc(pads_ready, 1)
                    dve.wait_ge(pads_ready, 2)
                for c in range(EARLY):
                    dve.wait_ge(early_hi_ready, c + 1)
                    dve.tensor_tensor(w_lo[:, c, :], w_raw[:, c % RAW, :], w_hi[:, c, :].bitcast(F32), ALU.subtract)\
                        .then_inc(early_ready, 1)
                    if c == 0:
                        front(0, 0, 0, list(AT))

                def copy_y(t):
                    dve.wait_ge(h_used, HB + t * NC)
                    dve.tensor_copy(yT[:, 1, :], y_ps[:, 1, :]).then_inc(y1_free, 1)

                def add_y(t, use):
                    dve.wait_ge(sum_loaded, 16 * t)
                    for half in range(2):
                        dve.wait_ge(t_full, use + half + 1)
                        xs = sum_sb[:, 2 * half:2 * half + 2, :]
                        dve.tensor_tensor(xs, xs, t_ps[:, :].rearrange("p (s d) -> p s d", d=D), ALU.add).then_inc(t_free, 1)

                def tile(i, q):
                    t = 2 * i + q
                    use = t * USES + FRONT
                    for c in range(NC):
                        g = t * NC + c
                        product(g, c, t)
                        if c >= 1 or not is_first(t):
                            hidden_lo(g - 1, (c - 1) % NC)
                        if c == 1 and not is_first(t):
                            copy_y(t)
                        if c == 2 and not is_first(t):
                            add_y(t, use - 2)
                        front(t + 1, 1 - q, use, front_steps(c))

                for q in range(2):
                    tile(0, q)
                with dve.Fori(1, TILES // 2) as i:
                    for q in range(2):
                        tile(i, q)
                hidden_lo(TILES * NC - 1, NC - 1)
                copy_y(TILES)
                add_y(TILES, TILES * USES + FRONT - 2)

        with nc.Block() as block:
            @block.sync
            def _(sp):
                for s in sems:
                    sp.sem_clear(s)


HEADS = 16
HD = D // HEADS
SEQ = 1024
BATCH = TOK // SEQ
QT = SEQ // P
VW = 32
BIG = -1e30


def project_phase(nc, name, x_in, w_qkv, b_qkv, q_dram, k_dram, v_sb, consts):
    ident, eps, neg_half = consts["ident"], consts["eps"], consts["neg_half"]
    biased = b_qkv is not None
    USES = KD
    with ExitStack() as ctx:
        def sb(n, shape, dt=F32):
            return ctx.enter_context(nc.sbuf_tensor(f"{name}_{n}", shape, dt))

        def ps(n, shape, dt=F32):
            return ctx.enter_context(nc.psum_tensor(f"{name}_{n}", shape, dt))

        sems = []

        def sem(n):
            sems.append(ctx.enter_context(nc.semaphore(f"{name}_{n}")))
            return sems[-1]

        w_raw = sb("w_raw", [P, 3, KD, D])
        w_hi = sb("w_hi", [P, 3, KD, D], F32R)
        w_lo = sb("w_lo", [P, 3, KD, D], F32R)
        x_sb = sb("x_sb", [P, 2, SUB, D])
        xn = sb("xn", [P, SUB, D])
        stats = sb("stats", [P, SUB, 6])
        moments = sb("moments", [P, SUB, 2])
        var_eps = sb("var_eps", [P, SUB])
        rstd = sb("rstd", [P, SUB])
        xT_hi = sb("xT_hi", [P, 2, KD, TILE], F32R)
        xT_lo = sb("xT_lo", [P, 2, KD, TILE], F32R)
        qk_hi = sb("qk_hi", [P, 2, 4, TILE], F32R)
        qk_lo = sb("qk_lo", [P, 2, 4, TILE], F32R)
        if biased:
            b_col = sb("b_col", [P, 4])
            bv_row = sb("bv_row", [P, D])
        t_ps = ps("t_ps", [P, TILE])
        qk_ps = ps("qk_ps", [P, 4, TILE])
        v_ps = ps("v_ps", [P, 2, 2, D])

        x_loaded = [sem("x_loaded0"), sem("x_loaded1")]
        w_loaded = sem("w_loaded")
        passed = sem("passed")
        b_loaded = sem("b_loaded")
        w_hi_ready = sem("w_hi_ready")
        w_ready = sem("w_ready")
        ones_ready = sem("ones_ready")
        stats_done = sem("stats_done")
        moments_done = sem("moments_done")
        var_done = sem("var_done")
        rstd_ready = sem("rstd_ready")
        xn_ready = sem("xn_ready")
        xh_ready = sem("xh_ready")
        t_full = sem("t_full")
        t_free = sem("t_free")
        qk_full = sem("qk_full")
        qk_hi_ready = sem("qk_hi_ready")
        qk_ready = sem("qk_ready")
        qk_stored = [sem("qk_stored0"), sem("qk_stored1")]
        v_full = sem("v_full")
        v_ready = sem("v_ready")

        x_in_v = x_in.rearrange("(t s p) d -> t p s d", p=P, s=SUB)
        v_v = v_sb[:, :].rearrange("p (b h k w) -> p b h k w", b=BATCH, h=HEADS, k=QT)

        with nc.Block() as block:

            @block.sync
            def _(sp):
                def load(t, p):
                    sp.dma_start(x_sb[:, p, :, :], x_in_v[t, :, :, :]).then_inc(x_loaded[p], 16)

                for p in range(2):
                    sp.sem_inc(qk_stored[p], 128)
                load(0, 0)
                for n, w in enumerate(w_qkv):
                    sp.dma_start(w_raw[:, n, :, :], w.rearrange("(k p) o -> p k o", p=P)).then_inc(w_loaded, 16)
                load(1, 1)
                if biased:
                    for n in range(2):
                        sp.dma_start(b_col[:, 2 * n:2 * n + 2], b_qkv[n].rearrange("(m p) -> p m", p=P),
                                     allow_slow_non_contiguous=True)\
                            .then_inc(b_loaded, 16)
                    sp.dma_start(bv_row[:, :], b_qkv[2].rearrange("(a d) -> a d", a=1).to_broadcast([P, D]))\
                        .then_inc(b_loaded, 16)
                with sp.Fori(0, TILES // 2) as i:
                    for p in range(2):
                        t = 2 * i + p
                        sp.wait_ge(xn_ready, t + 1)
                        load((t + 2) % TILES, p)
                        for m in range(4):
                            dram = (q_dram, k_dram)[m // 2]
                            heads = slice((m % 2) * 8, (m % 2) * 8 + 8)
                            sp.wait_ge(qk_ready, t * 4 + m + 5)
                            for l, part in enumerate((qk_hi, qk_lo)):
                                sp.dma_start(dram[i, heads, l, :, p * TILE:(p + 1) * TILE],
                                             part[:, p, m, :].bitcast(F32)).then_inc(qk_stored[p], 16)
                for p in range(2):
                    sp.wait_ge(x_loaded[p], 16 * (TILES // 2 + 1))
                    sp.wait_ge(qk_stored[p], 128 * (TILES // 2 + 1))

            @block.gpsimd
            def _(pool):
                def rstd_of(n):
                    pool.wait_ge(moments_done, n + 1)
                    pool.tensor_tensor(var_eps[:, :], moments[:, :, 1], eps[:, :], ALU.add).then_inc(var_done, 1)
                    pool.wait_ge(var_done, n + 1)
                    pool.tensor_tensor(rstd[:, :], var_eps[:, :], neg_half[:, :], ALU.pow).then_inc(rstd_ready, 1)

                rstd_of(0)
                pads = v_sb[:, :].rearrange("p (n w) -> p n w", w=VW)
                pool.memset(pads[:, :, HD:VW], 0.0).then_inc(ones_ready, 1)
                pool.wait_ge(ones_ready, 1)
                pool.memset(pads[:, :, HD], 1.0).then_inc(ones_ready, 1)
                with pool.Fori(1, TILES + 1) as n:
                    rstd_of(n)

            @block.tensor
            def _(pe):
                def split_mms(out, pairs):
                    for n, (a, b) in enumerate(pairs):
                        last = pe.matmul(out, a, b, start=(n == 0), stop=(n == len(pairs) - 1))
                    return last

                def x_turn(n, use, kd):
                    if kd == 0:
                        pe.wait_ge(xn_ready, n + 1)
                    if not isinstance(use, int) or use + kd > 0:
                        pe.wait_ge(t_free, use + kd)
                    for s in range(SUB):
                        last = pe.transpose(t_ps[:, s * P:(s + 1) * P], xn[:, s, kd * P:(kd + 1) * P], ident[:, :])
                    last.then_inc(t_full, 1)

                x_turn(0, 0, 0)
                x_turn(0, 0, 1)
                pe.wait_ge(w_ready, 3)
                with pe.Fori(0, TILES // 2) as i:
                    for q in range(2):
                        t = 2 * i + q
                        use = (t + 1) * USES
                        pe.wait_ge(t_free, use)
                        for m in range(4):
                            pe.wait_ge(qk_ready, t * 4 + m + 1)
                            n, cols = m // 2, slice((m % 2) * P, (m % 2 + 1) * P)
                            pairs = []
                            for kd in range(KD):
                                pairs += [(w_hi[:, n, kd, cols], xT_hi[:, q, kd, :]), (w_hi[:, n, kd, cols], xT_lo[:, q, kd, :]),
                                          (w_lo[:, n, kd, cols], xT_hi[:, q, kd, :])]
                            split_mms(qk_ps[:, m, :], pairs).then_inc(qk_full, 1)
                            if m >= 2:
                                x_turn(t + 1, use, m - 2)
                        for half in range(2):
                            pe.wait_ge(v_ready, t * 2 + half + 1)
                            for s in range(2):
                                toks = slice((2 * half + s) * P, (2 * half + s + 1) * P)
                                pairs = []
                                for kd in range(KD):
                                    pairs += [(xT_hi[:, q, kd, toks], w_hi[:, 2, kd, :]), (xT_hi[:, q, kd, toks], w_lo[:, 2, kd, :]),
                                              (xT_lo[:, q, kd, toks], w_hi[:, 2, kd, :])]
                                last = split_mms(v_ps[:, half, s, :], pairs)
                            last.then_inc(v_full, 1)

            @block.scalar
            def _(act):
                def x_hi(n, q, use, kd):
                    act.wait_ge(t_full, use + kd + 1)
                    act.activation(xT_hi[:, q, kd, :], t_ps[:, :], ACT.Copy).then_inc(xh_ready, 1)

                for n in range(3):
                    act.wait_ge(w_loaded, 48)
                    act.activation(w_hi[:, n, :, :], w_raw[:, n, :, :], ACT.Copy).then_inc(w_hi_ready, 1)
                x_hi(0, 0, 0, 0)
                x_hi(0, 0, 0, 1)
                if biased:
                    act.wait_ge(b_loaded, 48)
                with act.Fori(0, TILES // 2) as i:
                    for q in range(2):
                        t = 2 * i + q
                        for m in range(4):
                            act.wait_ge(qk_full, t * 4 + m + 1)
                            act.wait_ge(qk_stored[q], i * 128 + 128)
                            if biased:
                                act.activation(qk_hi[:, q, m, :], qk_ps[:, m, :], ACT.Identity, bias=b_col[:, m:m + 1])\
                                    .then_inc(qk_hi_ready, 1)
                            else:
                                act.activation(qk_hi[:, q, m, :], qk_ps[:, m, :], ACT.Copy).then_inc(qk_hi_ready, 1)
                            if m >= 2:
                                x_hi(t + 1, 1 - q, (t + 1) * USES, m - 2)

            @block.vector
            def _(dve):
                def find_moments(n, q, n_q):
                    dve.wait_ge(x_loaded[q], 16 * n_q)
                    layer_norm_moments(dve, x_sb[:, q, :, :], stats, moments, stats_done, moments_done, passed, n)

                def normalise(n, q):
                    dve.wait_ge(rstd_ready, n + 1)
                    for s in range(SUB):
                        last = dve.tensor_scalar(xn[:, s, :], x_sb[:, q, s, :], moments[:, s, 0:1], rstd[:, s:s + 1],
                                                 ALU.subtract, ALU.mult)
                    last.then_inc(xn_ready, 1)

                def x_lo(n, q, kd):
                    dve.wait_ge(xh_ready, 2 * n + kd + 1)
                    dve.tensor_tensor(xT_lo[:, q, kd, :], t_ps[:, :], xT_hi[:, q, kd, :].bitcast(F32),
                                      ALU.subtract).then_inc(t_free, 1)

                dve.sem_inc(v_ready, 2)
                dve.sem_inc(qk_ready, 4)
                find_moments(0, 0, 1)
                normalise(0, 0)
                for n in range(3):
                    dve.wait_ge(w_hi_ready, n + 1)
                    dve.tensor_tensor(w_lo[:, n, :, :], w_raw[:, n, :, :], w_hi[:, n, :, :].bitcast(F32), ALU.subtract)\
                        .then_inc(w_ready, 1)
                x_lo(0, 0, 0)
                x_lo(0, 0, 1)
                if biased:
                    dve.wait_ge(b_loaded, 48)
                with dve.Fori(0, TILES // 2) as i:
                    for q in range(2):
                        t = 2 * i + q
                        find_moments(t + 1, 1 - q, i + 1 + q)
                        for m in range(4):
                            dve.wait_ge(qk_hi_ready, t * 4 + m + 1)
                            hi = qk_hi[:, q, m, :].bitcast(F32)
                            if biased:
                                dve.scalar_tensor_tensor(out=qk_lo[:, q, m, :], in0=qk_ps[:, m, :], scalar=b_col[:, m:m + 1],
                                                         in1=hi, op0=ALU.add, op1=ALU.subtract).then_inc(qk_ready, 1)
                            else:
                                dve.tensor_tensor(qk_lo[:, q, m, :], qk_ps[:, m, :], hi, ALU.subtract).then_inc(qk_ready, 1)
                            if m == 0:
                                normalise(t + 1, 1 - q)
                            if m >= 2:
                                x_lo(t + 1, 1 - q, m - 2)
                        for half in range(2):
                            dve.wait_ge(v_full, t * 2 + half + 1)
                            for s in range(2):
                                src = v_ps[:, half, s, :].rearrange("p (h d) -> p h d", h=HEADS)
                                dst = v_v[:, i, :, q * SUB + 2 * half + s, 0:HD]
                                if biased:
                                    last = dve.tensor_tensor(dst, src, bv_row[:, :].rearrange("p (h d) -> p h d", h=HEADS), ALU.add)
                                else:
                                    last = dve.tensor_copy(dst, src)
                            last.then_inc(v_ready, 1)

        with nc.Block() as block:
            @block.sync
            def _(sp):
                for s in sems:
                    sp.sem_clear(s)


def piece_list(width):
    n = -(-width // TILE)
    cuts = [-(-width * k // (n * P)) * P for k in range(n + 1)]
    return [(a, b - a) for a, b in zip(cuts, cuts[1:])]


def heads_phase(nc, name, q_dram, k_dram, v_sb, o_sb, consts):
    identb, maskb, ident = consts["identb"], consts["maskb"], consts["ident"]
    R = 4
    N = BATCH * HEADS
    ROWS = 4 * HD
    OFF = [sum(SEQ - k * P for k in range(j)) for j in range(QT + 1)]
    PIECES = [piece_list(SEQ - j * P) for j in range(QT)]
    FIRST = [sum(len(PIECES[k]) for k in range(j)) for j in range(QT + 1)]
    NP = FIRST[QT]
    NB = 3
    assert NP % NB == 0
    QUADS = P // VW
    CHUNK = SEQ // QUADS

    def turns_before(n):
        return max(2 * n - 1, n + 1) if isinstance(n, int) else n * 2 - 1

    def is_early(n):
        return isinstance(n, int) and n < 2

    HALF = TILE // P
    S_USES = [(i, a, w) for i in reversed(range(QT)) for a, w in piece_list((i + 1) * P)]
    NS = len(S_USES)
    assert NS % 2 == 0
    LOAD = 5 * 16
    with ExitStack() as ctx:
        def sb(n, shape, dt=F32):
            return ctx.enter_context(nc.sbuf_tensor(f"{name}_{n}", shape, dt))

        def ps(n, shape, dt=F32):
            return ctx.enter_context(nc.psum_tensor(f"{name}_{n}", shape, dt))

        sems = []

        def sem(n):
            sems.append(ctx.enter_context(nc.semaphore(f"{name}_{n}")))
            return sems[-1]

        q_st = sb("q_st", [P, R, SEQ], F32R)
        k_st = sb("k_st", [P, R, SEQ], F32R)
        v_st = sb("v_st", [P, R, QT * VW])
        row_max = sb("row_max", [P, 2, P])
        neg_hi = sb("neg_hi", [QT, R, P], F32R)
        neg_lo = sb("neg_lo", [QT, R, P], F32R)
        probs = sb("probs", [P, 2, OFF[QT]])
        oT = sb("oT", [P, 2, CHUNK])
        inv_sum = sb("inv_sum", [P, 2, 2, QUADS])
        s_ps = ps("s_ps", [P, 2, TILE])
        st_ps = ps("st_ps", [P, NB, TILE])
        o_ps = ps("o_ps", [P, 2, TILE])
        turn_ps = ps("turn_ps", [P, CHUNK])

        stack_loaded = [sem(f"stack_loaded{r}") for r in range(R)]
        v_loaded = [sem(f"v_loaded{r}") for r in range(R)]
        neg_loaded = [sem(f"neg_loaded{r}") for r in range(R)]
        ones_ready = sem("ones_ready")
        zeros_ready = sem("zeros_ready")
        s_full = sem("s_full")
        s_free = sem("s_free")
        max_ready = sem("max_ready")
        turn_full = sem("turn_full")
        turn_free = sem("turn_free")
        neg_hi_ready = sem("neg_hi_ready")
        st_full = sem("st_full")
        exp_done = sem("exp_done")
        masked = sem("masked")
        passed = sem("passed")
        pv_done = sem("pv_done")
        sum_ready = sem("sum_ready")
        o_free = sem("o_free")

        with nc.Block() as block:

            @block.sync
            def _(sp):
                def load(n, r):
                    q_v = q_dram[n, :, :, :].rearrange("l d t -> (l d) t")
                    k_v = k_dram[n, :, :, :].rearrange("l d t -> (l d) t")
                    for to, src in ((q_st[0:32, r, :], q_v), (q_st[32:64, r, :], q_v), (k_st[0:32, r, :], k_v),
                                    (k_st[32:48, r, :], k_v[HD:2 * HD, :]), (k_st[48:64, r, :], k_v[0:HD, :])):
                        sp.dma_start(to.bitcast(F32), src).then_inc(stack_loaded[r], 16)

                def load_v(n, r):
                    sp.dma_start(v_st[:, r, :], v_sb[:, bass.ds(n * QT * VW, QT * VW)]).then_inc(v_loaded[r], 16)

                def put_neg(r, turns):
                    sp.wait_ge(turn_free, turns)
                    for row, part in ((ROWS, neg_hi), (ROWS + 1, neg_lo)):
                        sp.dma_start(q_st[row:row + 1, r, :].bitcast(F32), part[:, r, :].bitcast(F32)).then_inc(neg_loaded[r], 16)

                load(0, 0)
                load(1, 1)
                load(2, 2)
                load_v(0, 0)
                put_neg(0, 1)
                def slot(g, r):
                    n = g * R + r
                    sp.wait_ge(exp_done, n * NP + NB)
                    load((n + 3) % N, (r + 3) % R)
                    sp.wait_ge(pv_done, n + 1)
                    load_v((n + 1) % N, (r + 1) % R)
                    put_neg((r + 1) % R, turns_before(n) + 1)

                for r in range(R):
                    slot(0, r)
                with sp.Fori(1, N // R) as g:
                    for r in range(R):
                        slot(g, r)
                for r in range(R):
                    sp.wait_ge(v_loaded[r], 16 * (N // R + (1 if r < 1 else 0)))
                    sp.wait_ge(stack_loaded[r], LOAD * (N // R + (1 if r < 3 else 0)))
                    sp.wait_ge(neg_loaded[r], 32 * (N // R + (1 if r < 1 else 0)))

            @block.gpsimd
            def _(pool):
                pool.memset(k_st[ROWS:ROWS + 2, :, :].bitcast(F32), 1.0).then_inc(ones_ready, 1)
                with pool.Fori(0, N // R) as g:
                    for r in range(R):
                        n = g * R + r
                        for j in range(QT):
                            wait_alone(pool, exp_done, n * NP + FIRST[j] + 1 + NB, passed)
                            d = probs[:, r % 2, OFF[j]:OFF[j] + P]
                            pool.affine_select(out=d, in_=d, compare_op=ALU.is_ge, fill=0.0, base=0, pattern=[[1, P]],
                                               channel_multiplier=-1).then_inc(masked, 1)

            @block.tensor
            def _(pe):
                def scores(n, r, i):
                    for k, (block, a, w) in enumerate(S_USES):
                        if block != i:
                            continue
                        pe.wait_ge(s_free, n * NS + k + 1)
                        diag = a + w == (i + 1) * P
                        last = pe.matmul(s_ps[:, k % 2, 0:w], q_st[0:ROWS, r, i * P:(i + 1) * P], k_st[0:ROWS, r, a:a + w],
                                         start=True, stop=not diag)
                        if diag:
                            last = pe.matmul(s_ps[:, k % 2, w - P:w], identb[:, :], maskb[:, :], start=False, stop=True)
                        last.then_inc(s_full, 1)

                def max_turn(n, r, turns):
                    pe.wait_ge(max_ready, n + 1)
                    if turns is not None:
                        pe.wait_ge(turn_free, turns)
                    pe.transpose(turn_ps[:, 0:P], row_max[:, r % 2, :], ident[:, :]).then_inc(turn_full, 1)

                def out_turn(n, r, turns):
                    pe.wait_ge(o_free, n + 3)
                    pe.wait_ge(turn_free, turns)
                    for s in range(CHUNK // P):
                        last = pe.transpose(turn_ps[:, s * P:(s + 1) * P], oT[:, r % 2, s * P:(s + 1) * P], ident[:, :])
                    last.then_inc(turn_full, 1)

                def scores_t(n, r, j):
                    for k, (a, w) in enumerate(PIECES[j]):
                        u = FIRST[j] + k
                        pe.wait_ge(exp_done, n * NP + u + 1)
                        last = pe.matmul(st_ps[:, u % NB, 0:w], k_st[0:ROWS + 2, r, j * P:(j + 1) * P],
                                         q_st[0:ROWS + 2, r, j * P + a:j * P + a + w], start=True, stop=True)
                        last.then_inc(st_full, 1)

                def times_v(n, g, r, j):
                    if j == 0:
                        pe.wait_ge(v_loaded[r], 16 * (g + 1))
                        pe.wait_ge(o_free, n + 1)
                    pe.wait_ge(exp_done, n * NP + FIRST[j + 1] + NB)
                    pe.wait_ge(masked, n * QT + j + 1)
                    for c in reversed(range(QUADS)):
                        start = max(c * CHUNK, j * P)
                        width = (c + 1) * CHUNK - start
                        if width <= 0:
                            continue
                        at = OFF[j] + start - j * P
                        last = pe.matmul(o_ps[c * VW:(c + 1) * VW, r % 2, CHUNK - width:CHUNK], v_st[:, r, j * VW:(j + 1) * VW],
                                         probs[:, r % 2, at:at + width], start=(j == 0), stop=((j + 1) * P == (c + 1) * CHUNK))
                    if j == QT - 1:
                        last.then_inc(pv_done, 1)

                pe.sem_inc(pv_done, 2)
                pe.wait_ge(ones_ready, 1)
                pe.wait_ge(zeros_ready, 1)
                for n in range(2):
                    pe.wait_ge(stack_loaded[n], LOAD)
                    for i in reversed(range(QT)):
                        scores(n, n, i)
                    if n == 0:
                        max_turn(0, 0, None)

                def slot(g, r):
                    n = g * R + r
                    r2 = (r + 2) % R
                    pe.wait_ge(stack_loaded[r2], LOAD * (g + 1 + (r + 2) // R))
                    pe.wait_ge(neg_loaded[r], 32 * (g + 1))
                    for j in range(QT):
                        scores_t(n, r, j)
                        scores(n + 2, r2, QT - 1 - j)
                        if not is_first(n) and j % 2:
                            for block in (j - 1, j):
                                times_v(n - 1, g if r else g - 1, (r - 1) % R, block)
                        if j == 1:
                            max_turn(n + 1, (r + 1) % R, turns_before(n))
                        if j == 5 and not is_early(n):
                            out_turn(n - 2, r % 2, turns_before(n) + 1)

                for r in range(R):
                    slot(0, r)
                with pe.Fori(1, N // R) as g:
                    for r in range(R):
                        slot(g, r)
                for j in range(QT):
                    times_v(N - 1, N // R - 1, R - 1, j)
                for n in (N - 2, N - 1):
                    out_turn(n, n % 2, turns_before(N) + n - (N - 2))

            @block.scalar
            def _(act):
                def copy_out(n, r):
                    act.wait_ge(pv_done, n + 3)
                    if not is_early(n):
                        act.wait_ge(turn_free, n * 2 + 1)
                    act.activation(oT[:, r % 2, :], o_ps[:, r % 2, 0:CHUNK], ACT.Copy).then_inc(o_free, 1)

                def slot(g, r):
                    n = g * R + r
                    act.wait_ge(pv_done, n + 1)
                    for j in range(QT):
                        for k, (a, w) in enumerate(PIECES[j]):
                            u = FIRST[j] + k
                            act.wait_ge(st_full, n * NP + u + 1)
                            act.activation(probs[:, r % 2, OFF[j] + a:OFF[j] + a + w], st_ps[:, u % NB, 0:w], ACT.Exp,
                                           scale=float(HD) ** -0.5).then_inc(exp_done, 1)
                        if j == 2 and not is_early(n):
                            copy_out(n - 2, r)

                act.sem_inc(exp_done, NB)
                act.sem_inc(o_free, 2)
                for r in range(R):
                    slot(0, r)
                with act.Fori(1, N // R) as g:
                    for r in range(R):
                        slot(g, r)
                for n in (N - 2, N - 1):
                    copy_out(n, n % 2)

            @block.vector
            def _(dve):
                def reduce(n, r, i):
                    for k, (block, a, w) in enumerate(S_USES):
                        if block != i:
                            continue
                        dve.wait_ge(s_full, n * NS + k + 1)
                        col = i if a == 0 else QT + i - HALF
                        dve.tensor_reduce(row_max[:, r % 2, col:col + 1], s_ps[:, k % 2, 0:w], AX.X, ALU.max).then_inc(s_free, 1)
                    if i == 0:
                        dve.wait_ge(s_free, (n + 1) * NS + 2)
                        dve.tensor_tensor(row_max[:, r % 2, HALF:QT], row_max[:, r % 2, HALF:QT], row_max[:, r % 2, QT:QT + HALF],
                                          ALU.max).then_inc(max_ready, 1)

                def negate(n, r, turns):
                    dve.wait_ge(turn_full, turns)
                    dve.tensor_scalar(neg_hi[:, r, :], turn_ps[0:QT, 0:P], -1.0, None, ALU.mult).then_inc(neg_hi_ready, 1)
                    dve.wait_ge(neg_hi_ready, n + 1)
                    dve.scalar_tensor_tensor(out=neg_lo[:, r, :], in0=turn_ps[0:QT, 0:P], scalar=-1.0,
                                             in1=neg_hi[:, r, :].bitcast(F32), op0=ALU.mult, op1=ALU.subtract)\
                        .then_inc(turn_free, 1)

                def output(n, r, turns):
                    out = turn_ps[:, :].rearrange("p (s c w) -> p s c w", s=2, w=VW)
                    dst = o_sb[:, bass.ds(n * QT * HD, QT * HD)].rearrange("p (c s d) -> p s c d", s=2, d=HD)
                    dve.wait_ge(turn_full, turns)
                    dve.wait_ge(turn_free, turns - 1)
                    dve.reciprocal(inv_sum[:, r % 2, :, :], out[:, :, :, HD]).then_inc(sum_ready, 1)
                    dve.wait_ge(sum_ready, n + 1)
                    for s in range(2):
                        last = dve.tensor_tensor(dst[:, s, :, :], out[:, s, :, 0:HD],
                                                 inv_sum[:, r % 2, s, :].unsqueeze(2).to_broadcast([P, QUADS, HD]), ALU.mult)
                    last.then_inc(turn_free, 1)

                dve.sem_inc(s_free, 2)
                dve.memset(row_max[:, :, :], 0.0).then_inc(zeros_ready, 1)
                dve.wait_ge(zeros_ready, 1)
                for n in range(2):
                    for i in reversed(range(QT)):
                        reduce(n, n, i)
                    if n == 0:
                        negate(0, 0, 1)

                def slot(g, r):
                    n = g * R + r
                    for j in range(QT):
                        reduce(n + 2, (r + 2) % R, QT - 1 - j)
                        if j == 1:
                            negate(n + 1, (r + 1) % R, turns_before(n) + 1)
                        if j == 5 and not is_early(n):
                            output(n - 2, r, turns_before(n) + 2)

                for r in range(R):
                    slot(0, r)
                with dve.Fori(1, N // R) as g:
                    for r in range(R):
                        slot(g, r)
                for n in (N - 2, N - 1):
                    output(n, n % R, turns_before(N) + n - (N - 2) + 1)

        with nc.Block() as block:
            @block.sync
            def _(sp):
                for s in sems:
                    sp.sem_clear(s)


def out_phase(nc, name, o_sb, x_in, x_out, w_o, b_o, consts):
    ident = consts["ident"]
    biased = b_o is not None
    with ExitStack() as ctx:
        def sb(n, shape, dt=F32):
            return ctx.enter_context(nc.sbuf_tensor(f"{name}_{n}", shape, dt))

        def ps(n, shape, dt=F32):
            return ctx.enter_context(nc.psum_tensor(f"{name}_{n}", shape, dt))

        sems = []

        def sem(n):
            sems.append(ctx.enter_context(nc.semaphore(f"{name}_{n}")))
            return sems[-1]

        w_raw = sb("w_raw", [P, KD, D])
        w_hi = sb("w_hi", [P, KD, D], F32R)
        w_lo = sb("w_lo", [P, KD, D], F32R)
        b_row = sb("b_row", [P, D])
        x_sb = sb("x_sb", [P, 2, SUB, D])
        o_tok = sb("o_tok", [P, 2, SUB, D])
        oT_hi = sb("oT_hi", [P, 2, KD, TILE], F32R)
        oT_lo = sb("oT_lo", [P, 2, KD, TILE], F32R)
        t_ps = ps("t_ps", [P, 2, TILE])
        y_ps = ps("y_ps", [P, 2, 2, D])

        x_loaded = [sem("x_loaded0"), sem("x_loaded1")]
        x_stored = [sem("x_stored0"), sem("x_stored1")]
        w_loaded = sem("w_loaded")
        passed = sem("passed")
        w_hi_ready = sem("w_hi_ready")
        w_ready = sem("w_ready")
        tok_ready = sem("tok_ready")
        xb_ready = sem("xb_ready")
        t_full = sem("t_full")
        oh_ready = sem("oh_ready")
        t_free = sem("t_free")
        y_full = sem("y_full")
        y_free = sem("y_free")

        x_in_v = x_in.rearrange("(t s p) d -> t p s d", p=P, s=SUB)
        x_out_v = x_out.rearrange("(t s p) d -> t p s d", p=P, s=SUB)
        o_v = o_sb[:, :].rearrange("p (b h q d) -> p b h q d", b=BATCH, h=HEADS, q=QT)

        with nc.Block() as block:

            @block.sync
            def _(sp):
                def load(t, p):
                    sp.dma_start(x_sb[:, p, :, :], x_in_v[t, :, :, :]).then_inc(x_loaded[p], 16)

                sp.dma_start(w_raw[:, :, :], w_o.rearrange("(k p) o -> p k o", p=P)).then_inc(w_loaded, 16)
                if biased:
                    sp.dma_start(b_row[:, :], b_o.rearrange("(a d) -> a d", a=1).to_broadcast([P, D])).then_inc(w_loaded, 16)
                load(0, 0)
                load(1, 1)
                with sp.Fori(0, TILES // 2) as i:
                    for p in range(2):
                        t = 2 * i + p
                        sp.wait_ge(y_free, 2 * t + 4)
                        sp.dma_start(x_out_v[t, :, :, :], x_sb[:, p, :, :]).then_inc(x_stored[p], 16)
                        sp.wait_ge(x_stored[p], 16 * i + 16)
                        load((t + 2) % TILES, p)
                for p in range(2):
                    sp.wait_ge(x_loaded[p], 16 * (TILES // 2 + 1))

            @block.gpsimd
            def _(pool):
                with pool.Fori(0, TILES // 2) as i:
                    for q in range(2):
                        t = 2 * i + q
                        wait_alone(pool, t_free, 2 * t + 2, passed)
                        for s in range(SUB):
                            last = pool.tensor_copy(o_tok[:, q, s, :].rearrange("p (h d) -> p h d", h=HEADS),
                                                    o_v[:, i, :, q * SUB + s, :])
                        last.then_inc(tok_ready, 1)

            @block.tensor
            def _(pe):
                def split_mms(out, pairs):
                    for n, (a, b) in enumerate(pairs):
                        last = pe.matmul(out, a, b, start=(n == 0), stop=(n == len(pairs) - 1))
                    return last

                def turn(t, q):
                    pe.wait_ge(tok_ready, t + 1)
                    for kd in range(KD):
                        pe.wait_ge(t_free, 2 * t + kd + 3)
                        for s in range(SUB):
                            last = pe.transpose(t_ps[:, kd, s * P:(s + 1) * P], o_tok[:, q, s, kd * P:(kd + 1) * P], ident[:, :])
                        last.then_inc(t_full, 1)

                def project(t, q):
                    pe.wait_ge(t_free, 2 * t + 6)
                    for half in range(2):
                        pe.wait_ge(y_free, 2 * t + half + 1)
                        for s in range(2):
                            toks = slice((2 * half + s) * P, (2 * half + s + 1) * P)
                            pairs = []
                            for kd in range(KD):
                                pairs += [(oT_hi[:, q, kd, toks], w_hi[:, kd, :]), (oT_hi[:, q, kd, toks], w_lo[:, kd, :]),
                                          (oT_lo[:, q, kd, toks], w_hi[:, kd, :])]
                            last = split_mms(y_ps[:, half, s, :], pairs)
                        last.then_inc(y_full, 1)

                pe.wait_ge(w_ready, 1)
                turn(0, 0)
                with pe.Fori(0, TILES // 2 - 1) as i:
                    for q in range(2):
                        turn(2 * i + q + 1, 1 - q)
                        project(2 * i + q, q)
                turn(TILES - 1, 1)
                project(TILES - 2, 0)
                project(TILES - 1, 1)

            @block.scalar
            def _(act):
                act.wait_ge(w_loaded, 32 if biased else 16)
                act.activation(w_hi[:, :, :], w_raw[:, :, :], ACT.Copy).then_inc(w_hi_ready, 1)
                with act.Fori(0, TILES // 2) as i:
                    for q in range(2):
                        t = 2 * i + q
                        for kd in range(KD):
                            act.wait_ge(t_full, 2 * t + kd + 1)
                            act.activation(oT_hi[:, q, kd, :], t_ps[:, kd, :], ACT.Copy).then_inc(oh_ready, 1)

            @block.vector
            def _(dve):
                dve.sem_inc(t_free, 4)
                dve.sem_inc(y_free, 2)
                dve.wait_ge(w_hi_ready, 1)
                dve.tensor_tensor(w_lo[:, :, :], w_raw[:, :, :], w_hi[:, :, :].bitcast(F32), ALU.subtract).then_inc(w_ready, 1)

                def split(t, q):
                    for kd in range(KD):
                        dve.wait_ge(oh_ready, 2 * t + kd + 1)
                        dve.tensor_tensor(oT_lo[:, q, kd, :], t_ps[:, kd, :], oT_hi[:, q, kd, :].bitcast(F32),
                                          ALU.subtract).then_inc(t_free, 1)

                def add_bias(i, q):
                    if biased:
                        dve.wait_ge(x_loaded[q], 16 * i + 16)
                        for s in range(SUB):
                            last = dve.tensor_tensor(x_sb[:, q, s, :], x_sb[:, q, s, :], b_row[:, :], ALU.add)
                        last.then_inc(xb_ready, 1)

                def add_output(i, q):
                    t = 2 * i + q
                    for half in range(2):
                        dve.wait_ge(y_full, t * 2 + half + 1)
                        if biased:
                            dve.wait_ge(xb_ready, t + 1)
                        else:
                            dve.wait_ge(x_loaded[q], 16 * i + 16)
                        xs = x_sb[:, q, 2 * half:2 * half + 2, :]
                        dve.tensor_tensor(xs, xs, y_ps[:, half, :, :], ALU.add).then_inc(y_free, 1)

                split(0, 0)
                with dve.Fori(0, TILES // 2 - 1) as i:
                    for q in range(2):
                        split(2 * i + q + 1, 1 - q)
                        add_bias(i, q)
                        add_output(i, q)
                split(TILES - 1, 1)
                for q in range(2):
                    add_bias(TILES // 2 - 1, q)
                    add_output(TILES // 2 - 1, q)

        with nc.Block() as block:
            @block.sync
            def _(sp):
                for s in sems:
                    sp.sem_clear(s)


def make_constants(nc, ctx):
    def sb(n, shape, dt=F32):
        return ctx.enter_context(nc.sbuf_tensor(n, shape, dt))

    ident = sb("ident", [P, P])
    identb = sb("identb", [P, P], BF16)
    maskb = sb("maskb", [P, P], BF16)
    neg_half = sb("neg_half", [P, SUB])
    eps = sb("eps", [P, SUB])
    zeroed = ctx.enter_context(nc.semaphore("zeroed"))
    made = ctx.enter_context(nc.semaphore("made"))
    with nc.Block() as block:
        @block.gpsimd
        def _(pool):
            pool.memset(ident[:, :], 0.0).then_inc(zeroed, 1)
            pool.memset(identb[:, :], 0.0).then_inc(zeroed, 1)
            pool.memset(maskb[:, :], 0.0).then_inc(zeroed, 1)
            pool.memset(neg_half[:, :], -0.5).then_inc(zeroed, 1)
            pool.memset(eps[:, :], EPS).then_inc(zeroed, 1)
            pool.wait_ge(zeroed, 5)
            for m in (ident, identb):
                pool.affine_select(out=m[:, :], in_=m[:, :], compare_op=ALU.not_equal, fill=1.0, base=0,
                                   pattern=[[-1, P]], channel_multiplier=1).then_inc(made, 1)
            pool.affine_select(out=maskb[:, :], in_=maskb[:, :], compare_op=ALU.is_ge, fill=BIG, base=0,
                               pattern=[[-1, P]], channel_multiplier=1).then_inc(made, 1)
            pool.wait_ge(made, 3)
    return {"ident": ident, "identb": identb, "maskb": maskb, "eps": eps, "neg_half": neg_half}


def moe_phase(nc, name, x_in, x_out, w_router, we1, we3, we2, ws1, ws3, ws2, consts, lookup=None):
    HS = ws1.shape[1]

    def loads(c, raw):
        gate, up, down = (raw[:, k * D:(k + 1) * D] for k in range(3))
        cols = slice(c * P, (c + 1) * P)
        if c < HS // P:
            g_w, u_w, d_w = ws1[:, cols], ws3[:, cols], ws2[cols, :]
        else:
            e = c - HS // P
            g_w, u_w, d_w = we1[e, :, :], we3[e, :, :], we2[e, :, :]
        return [(gate.rearrange("p (k h) -> p k h", k=KD), g_w.rearrange("(k p) h -> p k h", p=P)),
                (up.rearrange("p (k h) -> p k h", k=KD), u_w.rearrange("(k p) h -> p k h", p=P)),
                (down, d_w)]

    ffn_phase(nc, name, x_in, x_out, HS // P + E, loads,
              {"shared": 0.5 / (TOP_K + 1), "routed": 0.5 * TOP_K / (TOP_K + 1)}, consts, w_router, lookup)


def lut_phase(nc, name, x_in, x_out, w_dram, chunks, consts):
    def loads(c, raw):
        return [(raw, w_dram[c, :, :])]

    ffn_phase(nc, name, x_in, x_out, chunks, loads, {"shared": 0.5}, consts)


def attention_phase(nc, name, x_in, x_out, q_dram, k_dram, w_qkv, b_qkv, w_o, b_o, consts):
    by_head = "b h l d t -> (b h) l d t"
    with nc.sbuf_tensor(f"{name}_o_sb", [P, BATCH * HEADS * QT * HD], F32) as o_sb:
        with nc.sbuf_tensor(f"{name}_v_sb", [P, BATCH * HEADS * QT * VW], F32) as v_sb:
            project_phase(nc, f"{name}_proj", x_in, w_qkv, b_qkv, q_dram, k_dram, v_sb, consts)
            heads_phase(nc, f"{name}_heads", q_dram.rearrange(by_head), k_dram.rearrange(by_head), v_sb, o_sb, consts)
        out_phase(nc, f"{name}_out", o_sb, x_in, x_out, w_o, b_o, consts)


def macaron(nc, t, out):
    def dram(name, shape, dt=F32):
        return nc.dram_tensor(name, shape, dt, kind="Internal").ap()

    INTER = t["L1_ffn_gate_idx"].shape[1]
    CHUNKS = -(-INTER // P)
    x1, x2, x3, x4, x5 = (dram(f"x{n}", [TOK, D]) for n in range(1, 6))
    q_dram = dram("q_dram", [BATCH, HEADS, 2, HD, SEQ])
    k_dram = dram("k_dram", [BATCH, HEADS, 2, HD, SEQ])
    w_dram = dram("w_dram", [CHUNKS, P, 3 * D])
    moe = [t[f"L0_ffn_{w}"] for w in ("w_router", "we1", "we3", "we2", "ws1", "ws3", "ws2")]
    with ExitStack() as ctx:
        pool_dma = [[ctx.enter_context(nc.semaphore(f"moe{m}_{n}")) for n in ("lut_loaded", "idx_loaded", "lookup_stored")]
                    for m in range(2)]
        parts = (range(0, CHUNKS // 2), range(CHUNKS // 2, CHUNKS))
        lookup = [(t["L1_ffn_lut"], [t[f"L1_ffn_{w}_idx"] for w in ("gate", "up", "down")], w_dram, part, dma)
                  for part, dma in zip(parts, pool_dma)]
        consts = make_constants(nc, ctx)
        moe_phase(nc, "moe0", t["L0_attn_x"], x1, *moe, consts, lookup[0])
        attention_phase(nc, "attn0", x1, x2, q_dram, k_dram, [t[f"L0_attn_W{w}"] for w in "qkv"],
                        [t[f"L0_attn_b{w}"] for w in "qkv"], t["L0_attn_Wo"], t["L0_attn_bo"], consts)
        moe_phase(nc, "moe1", x2, x3, *moe, consts, lookup[1])
        lut_phase(nc, "lut0", x3, x4, w_dram, CHUNKS, consts)
        attention_phase(nc, "attn1", x4, x5, q_dram, k_dram, [t[f"L1_attn_W{w}"] for w in "qkv"], None,
                        t["L1_attn_Wp"], None, consts)
        lut_phase(nc, "lut1", x5, out, w_dram, CHUNKS, consts)


_INS = ['L0_attn_x', 'L0_attn_Wq T', 'L0_attn_bq', 'L0_attn_Wk T', 'L0_attn_bk', 'L0_attn_Wv T', 'L0_attn_bv', 'L0_attn_Wo T',
        'L0_attn_bo', 'L0_ffn_w_router', 'L0_ffn_we1', 'L0_ffn_we3', 'L0_ffn_we2', 'L0_ffn_ws1', 'L0_ffn_ws3', 'L0_ffn_ws2',
        'L1_attn_Wq T', 'L1_attn_Wk T', 'L1_attn_Wv T', 'L1_attn_Wp T', 'L1_ffn_lut', 'L1_ffn_gate_idx T', 'L1_ffn_up_idx T',
        'L1_ffn_down_idx T']


def kernel(**inputs):
    import numpy as _np
    import concourse.bacc as _bacc
    from concourse import mybir as _mybir
    from concourse.bass_utils import run_bass_kernel_spmd as _run

    nc = _bacc.Bacc("TRN2", target_bir_lowering=False, num_devices=1)
    arrays, tensors = {}, {}
    shape = inputs['L0_attn_x'].shape
    for entry in _INS:
        name, _, turned = entry.partition(" ")
        a = _np.asarray(inputs[name])
        if turned:
            a = a.T
        if name == 'L0_attn_x':
            a = a.reshape(-1, a.shape[-1])
        a = _np.ascontiguousarray(a)
        arrays[f"in_{name}_dram"] = a
        tensors[name] = nc.dram_tensor(f"in_{name}_dram", a.shape, _mybir.dt.from_np(a.dtype), kind="ExternalInput").ap()
    out = nc.dram_tensor("out_0_dram", (TOK, D), _mybir.dt.from_np(_np.dtype("float32")), kind="ExternalOutput").ap()
    macaron(nc, tensors, out)
    r = _run(nc, [arrays], core_ids=[0])
    return r.results[0]["out_0_dram"].reshape(shape)
```
